# Optimizing a Trainium2 kernel written in Bass

```python
import numpy as np
import jax
import jax.numpy as jnp

def _softmax(x, axis=-1):
    return jax.nn.softmax(x, axis=axis)

def _gelu(x):
    return jax.nn.gelu(x, approximate=True)

def _silu(x):
    return jax.nn.silu(x)

def _sigmoid(x):
    return jax.nn.sigmoid(x)

def _layernorm(x, axis=-1, eps=1e-05):
    m = jnp.mean(x, axis=axis, keepdims=True)
    v = jnp.var(x, axis=axis, keepdims=True)
    return (x - m) / jnp.sqrt(v + eps)

def _scatter_add(tgt, idx, src, axis=0):
    return tgt.at[idx].add(src)

def _segment_sum(src, seg, n):
    return jax.ops.segment_sum(src, seg, n)
kernel_name = 'mk_cond_seq_d1_seqx_r4_96e6b1'

def setup_inputs(seed: int=0):
    np.random.seed(seed)
    _w = jnp.asarray

    def _rec_inputs():
        import jax
        import jax.numpy as jnp
        _rk = jax.random.key(seed)
        x = 7.22e-05 + 1 * jax.random.normal(jax.random.fold_in(_rk, 1), (8, 512, 256), jnp.float32)
        _lenS = 512 - jax.random.randint(jax.random.fold_in(_rk, 7), (8,), 0, max(1, 512 // 4) + 1, jnp.int32)
        _lenS2 = 512 - jax.random.randint(jax.random.fold_in(_rk, 8), (8,), 0, max(1, 512 // 4) + 1, jnp.int32)
        cond_1024 = 0.00782532 + 1.00527 * jax.random.normal(jax.random.fold_in(_rk, 11), (8, 256), jnp.float32)
        return (x, cond_1024)
    x, cond_1024 = _rec_inputs()

    def _L0_cond_setup():
        import jax, jax.numpy as jnp
        import numpy as np
        H = 256
        NH = 16
        DH = H // NH
        MLP = 4 * H
        EPS = 1e-05

        def _ln(x):
            m = jnp.mean(x, axis=-1, keepdims=True)
            v = jnp.mean((x - m) ** 2, axis=-1, keepdims=True)
            return (x - m) * jax.lax.rsqrt(v + EPS)

        def _modulate(x, shift, scale):
            return x * (1.0 + scale[:, None, :]) + shift[:, None, :]
        key = jax.random.key(seed)
        ks = jax.random.split(key, 12)
        s = 1.0 / np.sqrt(H)
        inp = {'x': jax.random.normal(ks[0], (8, 256, H), jnp.float32), 'c': jax.random.normal(ks[1], (8, H), jnp.float32), 'Wc': jax.random.normal(ks[2], (H, 6 * H), jnp.float32) * s, 'bc': jnp.zeros((6 * H,), jnp.float32), 'Wq': jax.random.normal(ks[3], (H, H), jnp.float32) * s, 'bq': jnp.zeros((H,), jnp.float32), 'Wk': jax.random.normal(ks[4], (H, H), jnp.float32) * s, 'bk': jnp.zeros((H,), jnp.float32), 'Wv': jax.random.normal(ks[5], (H, H), jnp.float32) * s, 'bv': jnp.zeros((H,), jnp.float32), 'Wo': jax.random.normal(ks[6], (H, H), jnp.float32) * s, 'bo': jnp.zeros((H,), jnp.float32), 'W1': jax.random.normal(ks[7], (H, MLP), jnp.float32) * s, 'b1': jnp.zeros((MLP,), jnp.float32), 'W2': jax.random.normal(ks[8], (MLP, H), jnp.float32) * (1.0 / np.sqrt(MLP)), 'b2': jnp.zeros((H,), jnp.float32)}
        return inp
    _L0_cond_all = _L0_cond_setup()
    _L0_cond_in = {k: v for k, v in _L0_cond_all.items() if k in ('Wc', 'bc', 'Wq', 'bq', 'Wk', 'bk', 'Wv', 'bv', 'Wo', 'bo', 'W1', 'b1', 'W2', 'b2')}
    del _L0_cond_all
    return {'x': x, 'cond_1024': cond_1024, 'L0_cond_Wc': _L0_cond_in['Wc'], 'L0_cond_bc': _L0_cond_in['bc'], 'L0_cond_Wq': _L0_cond_in['Wq'], 'L0_cond_bq': _L0_cond_in['bq'], 'L0_cond_Wk': _L0_cond_in['Wk'], 'L0_cond_bk': _L0_cond_in['bk'], 'L0_cond_Wv': _L0_cond_in['Wv'], 'L0_cond_bv': _L0_cond_in['bv'], 'L0_cond_Wo': _L0_cond_in['Wo'], 'L0_cond_bo': _L0_cond_in['bo'], 'L0_cond_W1': _L0_cond_in['W1'], 'L0_cond_b1': _L0_cond_in['b1'], 'L0_cond_W2': _L0_cond_in['W2'], 'L0_cond_b2': _L0_cond_in['b2']}

def reference(x, cond_1024, L0_cond_Wc, L0_cond_bc, L0_cond_Wq, L0_cond_bq, L0_cond_Wk, L0_cond_bk, L0_cond_Wv, L0_cond_bv, L0_cond_Wo, L0_cond_bo, L0_cond_W1, L0_cond_b1, L0_cond_W2, L0_cond_b2):
    import jax
    import jax.numpy as jnp

    def _L0_cond_ref(x, c, Wc, bc, Wq, bq, Wk, bk, Wv, bv, Wo, bo, W1, b1, W2, b2):
        import jax, jax.numpy as jnp
        import numpy as np
        H = 256
        NH = 16
        DH = H // NH
        MLP = 4 * H
        EPS = 1e-05

        def _ln(x):
            m = jnp.mean(x, axis=-1, keepdims=True)
            v = jnp.mean((x - m) ** 2, axis=-1, keepdims=True)
            return (x - m) * jax.lax.rsqrt(v + EPS)

        def _modulate(x, shift, scale):
            return x * (1.0 + scale[:, None, :]) + shift[:, None, :]
        B, S, _ = x.shape
        c6 = jax.nn.silu(c) @ Wc + bc
        sh_msa, sc_msa, g_msa, sh_mlp, sc_mlp, g_mlp = jnp.split(c6, 6, axis=-1)
        xm = _modulate(_ln(x), sh_msa, sc_msa)
        q = (xm @ Wq + bq).reshape(B, S, NH, DH)
        k = (xm @ Wk + bk).reshape(B, S, NH, DH)
        v = (xm @ Wv + bv).reshape(B, S, NH, DH)
        q = q / DH
        w = jnp.einsum('bqhc,bkhc->bhqk', q, k)
        w = jax.nn.softmax(w, axis=-1)
        y = jnp.einsum('bhqk,bkhc->bqhc', w, v).reshape(B, S, H)
        x = x + g_msa[:, None, :] * (y @ Wo + bo)
        xm2 = _modulate(_ln(x), sh_mlp, sc_mlp)
        h = jax.nn.gelu(xm2 @ W1 + b1, approximate=False)
        x = x + g_mlp[:, None, :] * (h @ W2 + b2)
        return x
    x = _L0_cond_ref(x, cond_1024, L0_cond_Wc, L0_cond_bc, L0_cond_Wq, L0_cond_bq, L0_cond_Wk, L0_cond_bk, L0_cond_Wv, L0_cond_bv, L0_cond_Wo, L0_cond_bo, L0_cond_W1, L0_cond_b1, L0_cond_W2, L0_cond_b2)
    return x

_drawn_inputs = setup_inputs


def setup_inputs(seed=0):
    import zlib

    import numpy as np

    out = dict(_drawn_inputs(seed))
    spreads = {'L0_cond_bc': (0.0, 0.1),
     'L0_cond_bq': (0.0, 2.0),
     'L0_cond_bk': (0.0, 2.0),
     'L0_cond_bv': (0.0, 0.1),
     'L0_cond_bo': (0.0, 0.1),
     'L0_cond_b1': (0.0, 0.1),
     'L0_cond_b2': (0.0, 0.1)}
    factors = {}
    for name, (base, spread) in spreads.items():
        noise = np.random.default_rng([zlib.crc32(name.encode()), seed]).standard_normal(out[name].shape)
        drawn = base * np.exp(spread * noise) if base else spread * noise
        out[name] = jnp.asarray(drawn.astype(out[name].dtype))
    for name, factor in factors.items():
        out[name] = (out[name] * factor).astype(out[name].dtype)
    return out
```

```python
from contextlib import ExitStack

import concourse.bass as bass
from concourse import mybir

F32 = mybir.dt.float32
F32R = mybir.dt.float32r
BF16 = mybir.dt.bfloat16
ALU = mybir.AluOpType
ACT = mybir.ActivationFunctionType
AXX = mybir.AxisListType.X

NB, S, H = 8, 512, 256
NH, DH = 16, 16
MLP = 4 * H
P = 128
KC = H // P
TT = S // P
JT = MLP // P
QPARTS = (0, 0, 1, 1, 0, 2)
KPARTS = (0, 1, 0, 1, 2, 0)
NSLOT = len(QPARTS)
MROW = NSLOT * DH
KROWS = MROW + 2
G = 4
NG = NH // G
STEPS = NG * TT
EPS = 1e-5
HB, HR = 2, 3
SH1, SC1, G1, SH2, SC2, G2 = range(6)


def dit_block(nc, x, c, Wc, bc, Wq, bq, Wk, bk, Wv, bv, Wo, bo, W1, b1, W2, b2, out,
              c6_scr, parts_scr, y_scr, r_scr):
    with ExitStack() as ctx:
        def sb(name, shape, dt=F32):
            return ctx.enter_context(nc.sbuf_tensor(name, shape, dt))

        def sem(name):
            return ctx.enter_context(nc.semaphore(name))

        ps = ctx.enter_context(nc.psum_tensor("ps", [P, 8, 512], F32))

        wqkvo = [sb(f"wqkvo_{n}", [P, 4, KC, H], F32R) for n in ("hi", "lo")]
        w1 = [sb(f"w1_{n}", [P, KC, MLP], F32R) for n in ("hi", "lo")]
        w2 = [sb(f"w2_{n}", [P, JT, H], F32R) for n in ("hi", "lo")]
        bo_b = sb("bo_b", [P, H])
        b2_b = sb("b2_b", [P, H])
        bias_t = sb("bias_t", [P, 3 * KC + JT])
        bqk = bias_t[:, 0:2 * KC].rearrange("p (n c) -> p n c", n=2)
        bv_t = bias_t[:, 2 * KC:3 * KC]
        b1_t = bias_t[:, 3 * KC:]
        ident = sb("ident", [P, P])
        mhalf = sb("mhalf", [P, TT])
        mod = sb("mod", [P, 12, NB])
        xa = sb("xa", [P, TT, H])
        xn = [xa, sb("xn2", [P, TT, H])]
        stats = [sb(f"stats{n}", [P, TT, 6]) for n in (1, 2)]
        mv = [sb(f"mv{n}", [P, TT, 2]) for n in (1, 2)]
        vare = [sb(f"vare{n}", [P, TT]) for n in (1, 2)]
        rstd = [sb(f"rstd{n}", [P, TT]) for n in (1, 2)]
        z1 = sb("z", [P, KC, S])
        z = [z1, z1]
        zh = [sb(f"zh{n}", [P, KC, S], F32R) for n in (1, 2)]
        zl = [sb(f"zl{n}", [P, KC, S], F32R) for n in (1, 2)]
        qst = [sb(f"qst{n}", [P, NH, S], BF16) for n in (0, 1)]
        kst = [sb(f"kst{n}", [P, NH, S], BF16) for n in (0, 1)]
        stage = qst[1][:].rearrange("p h s -> p (h s)").bitcast(F32).rearrange("p (n f) -> p n f", n=2)
        vaug = [sb(f"vaug{n}", [P, TT, NH, 2 * DH]) for n in (0, 1)]
        mx = sb("mx", [P, TT, NH])
        mrow = sb("mrow", [NH, 2, S], BF16)
        prob = sb("prob", [P, 2, G, S])
        prob_flat = prob[:].rearrange("p n g s -> p (n g s)")
        parts = prob_flat[:, 0:6 * S].bitcast(BF16).rearrange("p (j n s) -> p j n s", j=4, n=3)
        rest = prob_flat[:, 6 * S:8 * S].rearrange("p (n s) -> p n s", n=2)
        yc = sb("yc", [P, KC, S])
        rb = sb("rb", [P, KC, S])
        den = rb[0:NH, 0, :]
        rec = rb[0:NH, 1, :]
        ysb = rb
        yh, yl = zh[0], zl[0]
        ga = sb("ga", [P, H])
        gm = sb("gm", [P, H])
        gbias = yc[:, 0, 0:H]
        xd = sb("xd", [P, TT, H])
        x1 = sb("x1", [P, TT, H])
        hb = z1
        hh = sb("hh", [P, HR, S], F32R)
        hl = sb("hl", [P, HR, S], F32R)
        osb = xn[1]

        w_loaded, w_split, c6_loaded = sem("w_loaded"), sem("w_split"), sem("c6_loaded")
        c6_written = sem("c6_written")
        const_set, ident_set, prep_dve, prep_pe, prep_act = (
            sem("const_set"), sem("ident_set"), sem("prep_dve"), sem("prep_pe"), sem("prep_act"))
        xa_loaded = sem("xa_loaded")
        xd_loaded = sem("xd_loaded")
        ga_loaded = sem("ga_loaded")
        gm_loaded = sem("gm_loaded")
        stat_done = [sem(f"stat_done{n}") for n in (1, 2)]
        rstd_done = [sem(f"rstd_done{n}") for n in (1, 2)]
        xn_done = [sem(f"xn_done{n}") for n in (1, 2)]
        tp_done = [sem(f"tp_done{n}") for n in (1, 2)]
        z_done = [sem(f"z_done{n}") for n in (1, 2)]
        zh_done = [sem(f"zh_done{n}") for n in (1, 2)]
        zl_done = [sem(f"zl_done{n}") for n in (1, 2)]
        qk_done = sem("qk_done")
        part_h = sem("part_h")
        rest_done = sem("rest_done")
        part_m = sem("part_m")
        part_l = sem("part_l")
        parts_written = sem("parts_written")
        stack_loaded = sem("stack_loaded")
        v_done = sem("v_done")
        vaug_done = sem("vaug_done")
        s_done = sem("s_done")
        max_done = sem("max_done")
        mt_done = sem("mt_done")
        mrow_done = sem("mrow_done")
        m_loaded = sem("m_loaded")
        st_done = sem("st_done")
        exp_done = sem("exp_done")
        pv_done = sem("pv_done")
        y_evac = sem("y_evac")
        y_written = [sem(f"y_written{n}") for n in (0, 1)]
        yc_loaded = sem("yc_loaded")
        rec_done = sem("rec_done")
        r_written = sem("r_written")
        rb_loaded = sem("rb_loaded")
        yn_done = sem("yn_done")
        yh_done = sem("yh_done")
        yl_done = sem("yl_done")
        wo_done = sem("wo_done")
        gbo_done = sem("gbo_done")
        xg_done = sem("xg_done")
        x1_gated = sem("x1_gated")
        x1_done = sem("x1_done")
        gb2_done = sem("gb2_done")
        x1g_done = sem("x1g_done")
        w1_done = sem("w1_done")
        gelu_done = sem("gelu_done")
        hh_done = sem("hh_done")
        hl_done = sem("hl_done")
        w2_done = sem("w2_done")
        o_gated = sem("o_gated")
        o_done = sem("o_done")
        out_written = sem("out_written")

        def schedule(step, engine):
            for i in (-2, -1, 0, 1):
                step(i, i % 2)
            with engine.Fori(2, 5, 2) as i:
                step(i, 0)
                step(i + 1, 1)
            for i in (6, 7, 8):
                step(i, i % 2)

        def runs(i, lag):
            return not isinstance(i, int) or 0 <= i + lag < NB

        def later(i, lag, n):
            return not isinstance(i, int) or i + lag >= n

        block = ctx.enter_context(nc.Block())

        @block.sync
        def _(sp):
            sp.dma_start(stage[0:NB, 1, 0:H], c).then_inc(c6_loaded, 16)
            sp.dma_start(stage[0:NB, 1, 256:256 + 6 * H], bc.rearrange("(o f) -> o f", o=1).broadcast_to([NB, 6 * H]))\
                .then_inc(c6_loaded, 16)
            wc_sb = vaug[0][:].rearrange("p t h d -> p (t h d)")
            sp.dma_start(wc_sb[:, 0:1536], Wc[0:P, :]).then_inc(c6_loaded, 16)
            sp.dma_start(qst[0][:].rearrange("p h s -> p (h s)").bitcast(F32)[:, 0:1536], Wc[P:H, :]).then_inc(c6_loaded, 16)
            for n, w in enumerate((Wq, Wk, Wv, Wo)):
                sp.dma_start(stage[:, 0, n * 512:(n + 1) * 512].rearrange("p (c f) -> p c f", c=KC),
                             w.rearrange("(c p) f -> p c f", p=P)).then_inc(w_loaded, 16)
            sp.dma_start(kst[0][:].rearrange("p h s -> p (h s)").bitcast(F32)[:, 0:2048].rearrange("p (c f) -> p c f", c=KC),
                         W1.rearrange("(c p) f -> p c f", p=P)).then_inc(w_loaded, 16)
            sp.dma_start(kst[0][:].rearrange("p h s -> p (h s)").bitcast(F32)[:, 2048:4096].rearrange("p (c f) -> p c f", c=JT),
                         W2.rearrange("(c p) f -> p c f", p=P)).then_inc(w_loaded, 16)
            at = 0
            for b, rows in ((bq, KC), (bk, KC), (bv, KC), (b1, JT)):
                sp.dma_start(stage[at:at + rows, 1, 1792:1920], b.rearrange("(c p) -> c p", p=P)).then_inc(w_loaded, 16)
                at += rows
            for d, b in ((bo_b, bo), (b2_b, b2)):
                sp.dma_start(d[:], b.rearrange("(o f) -> o f", o=1).broadcast_to([P, H])).then_inc(w_loaded, 16)
            sp.wait_ge(prep_dve, 4)
            sp.dma_start(c6_scr[:], stage[0:NB, 1, 256:256 + 6 * H]).then_inc(c6_written, 16)
            sp.wait_ge(c6_written, 16)

            def step(i, par):
                if runs(i, 2):
                    b = i + 2
                    if later(i, 2, 1):
                        sp.wait_ge(tp_done[0], b)
                    sp.dma_start(xa[:], x[bass.ds(b, 1)].rearrange("o (t p) f -> p (o t) f", p=P)).then_inc(xa_loaded, 16)
                if runs(i, 0):
                    if later(i, 0, 1):
                        sp.wait_ge(x1_done, i)
                    sp.dma_start(xd[:], x[bass.ds(i, 1)].rearrange("o (t p) f -> p (o t) f", p=P)).then_inc(xd_loaded, 16)
                    sp.dma_start(ga[:], c6_scr[bass.ds(i, 1), G1 * H:(G1 + 1) * H].broadcast_to([P, H])).then_inc(ga_loaded, 16)
                if runs(i, -1):
                    if later(i, -1, 1):
                        sp.wait_ge(o_gated, i - 1)
                    sp.dma_start(gm[:], c6_scr[bass.ds(i - 1, 1), G2 * H:(G2 + 1) * H].broadcast_to([P, H])).then_inc(gm_loaded, 16)
                if runs(i, 1):
                    b = i + 1
                    sp.wait_ge(mrow_done, 2 * b + 2)
                    for n in range(2):
                        sp.dma_start(qst[1 - par][MROW + n:MROW + n + 1, :, :],
                                     mrow[:, n, :]).then_inc(m_loaded, 16)
                if runs(i, 2):
                    b = i + 2
                    for j in range(4):
                        sp.wait_ge(part_l, 4 * b + j + 1)
                        m = j % 2
                        sp.dma_start(parts_scr[j // 2, :, m * P:(m + 1) * P, :].rearrange("n p s -> p n s"),
                                     parts[:, j, :, :]).then_inc(parts_written, 16)
                    sp.wait_ge(parts_written, 64 * b + 64)
                    if later(i, 2, 2):
                        sp.wait_ge(st_done, 32 * b - 32)
                    for w, (stk, which) in enumerate(((qst, QPARTS), (kst, KPARTS))):
                        for slot, part in enumerate(which):
                            sp.dma_start(stk[par][slot * DH:(slot + 1) * DH, :, :],
                                         parts_scr[w, part].rearrange("(h d) s -> d h s", d=DH)).then_inc(stack_loaded, 16)
                if runs(i, -1):
                    sp.wait_ge(o_done, i)
                    sp.dma_start(out[bass.ds(i - 1, 1)].rearrange("o (t p) f -> p (o t) f", p=P), osb[:]).then_inc(out_written, 16)

            schedule(step, sp)
            sp.wait_ge(out_written, 16 * NB)

        @block.gpsimd
        def _(pool):
            pool.memset(ident[:], 0.0).then_inc(ident_set, 1)
            pool.wait_ge(ident_set, 1)
            pool.affine_select(out=ident[:], in_=ident[:], compare_op=ALU.not_equal, fill=1.0, base=0,
                               pattern=[[-1, P]], channel_multiplier=1).then_inc(ident_set, 1)
            pool.memset(mhalf[:], -0.5).then_inc(const_set, 1)
            pool.wait_ge(const_set, 1)
            pool.memset(kst[1][MROW:KROWS, :, :], -1.0).then_inc(const_set, 1)
            pool.wait_ge(const_set, 2)
            pool.memset(vaug[1][:, :, :, DH:], 1.0).then_inc(const_set, 1)
            pool.wait_ge(w_split, 1)
            pool.tensor_tensor(wqkvo[1][:].rearrange("p n c f -> p (n c f)"), stage[:, 0, :],
                               wqkvo[0][:].rearrange("p n c f -> p (n c f)").bitcast(F32), ALU.subtract).then_inc(const_set, 1)
            kf = kst[0][:].rearrange("p h s -> p (h s)").bitcast(F32)
            pool.wait_ge(w_split, 3)
            pool.tensor_tensor(w1[1][:].rearrange("p c f -> p (c f)"), kf[:, 0:2048],
                               w1[0][:].rearrange("p c f -> p (c f)").bitcast(F32), ALU.subtract).then_inc(const_set, 1)
            pool.tensor_tensor(w2[1][:].rearrange("p c f -> p (c f)"), kf[:, 2048:4096],
                               w2[0][:].rearrange("p c f -> p (c f)").bitcast(F32), ALU.subtract).then_inc(const_set, 1)
            pool.wait_ge(const_set, 6)
            pool.memset(kst[0][MROW:KROWS, :, :], -1.0).then_inc(const_set, 1)
            pool.wait_ge(const_set, 7)
            pool.wait_ge(prep_pe, 2)
            pool.memset(vaug[0][:, :, :, DH:], 1.0).then_inc(const_set, 1)

            def norm(n, b):
                pool.wait_ge(stat_done[n], 3 * b + 3)
                pool.tensor_tensor(rstd[n][:], vare[n][:], mhalf[:], ALU.pow).then_inc(rstd_done[n], 1)

            def z_lo(n, b):
                pool.wait_ge(zh_done[n], b + 1)
                pool.tensor_tensor(zl[n][:], z[n][:], zh[n][:].bitcast(F32), ALU.subtract).then_inc(zl_done[n], 1)

            def step(i, par):
                if runs(i, -1):
                    norm(1, i - 1)
                if runs(i, 2):
                    norm(0, i + 2)
                if runs(i, -1):
                    pool.wait_ge(gm_loaded, 16 * i)
                    pool.wait_ge(yh_done, i)
                    pool.wait_ge(yl_done, i)
                    pool.tensor_tensor(gbias, gm[:], b2_b[:], ALU.mult).then_inc(gb2_done, 1)
                    pool.wait_ge(gb2_done, i)
                    pool.wait_ge(xn_done[1], i)
                    pool.tensor_tensor(x1[:], x1[:], gbias.unsqueeze(1).broadcast_to([P, TT, H]), ALU.add).then_inc(x1g_done, 1)
                if runs(i, 0):
                    pool.wait_ge(ga_loaded, 16 * i + 16)
                    if later(i, 0, 1):
                        pool.wait_ge(x1g_done, i)
                    pool.tensor_tensor(gbias, ga[:], bo_b[:], ALU.mult).then_inc(gbo_done, 1)
                    pool.wait_ge(gbo_done, i + 1)
                    pool.wait_ge(xd_loaded, 16 * i + 16)
                    pool.tensor_tensor(xd[:], xd[:], gbias.unsqueeze(1).broadcast_to([P, TT, H]), ALU.add).then_inc(xg_done, 1)
                if runs(i, 2):
                    z_lo(0, i + 2)
                if runs(i, -1):
                    z_lo(1, i - 1)
                if runs(i, 2):
                    b = i + 2
                    for j in range(4):
                        pool.wait_ge(part_m, 4 * b + j + 1)
                        pool.tensor_tensor(parts[:, j, 2, :], rest[:, j % 2, :], parts[:, j, 1, :], ALU.subtract).then_inc(part_l, 1)
                if runs(i, -1):
                    b = i - 1
                    for j in range(JT):
                        pool.wait_ge(hh_done, JT * b + j + 1)
                        pool.tensor_tensor(hl[:, j % HR, :], hb[:, j % HB, :], hh[:, j % HR, :].bitcast(F32), ALU.subtract).then_inc(hl_done, 1)

            schedule(step, pool)

        @block.scalar
        def _(act):
            act.wait_ge(prep_pe, 1)
            act.activation(z[0][:, 0, 0:KC * NB], ps[:, 0, 0:KC * NB], ACT.Exp, scale=-1.0).then_inc(prep_act, 1)

            def modulate(n, b, banks, shift, scale):
                act.wait_ge(tp_done[n], b + 1)
                if n == 1 and later(b, 3, 3) and (not isinstance(b, int) or b + 3 < NB):
                    act.wait_ge(zl_done[0], b + 4)
                if n == 0 and later(b, -4, 0):
                    act.wait_ge(hl_done, JT * (b - 3))
                if n == 1 and later(b, -1, 0):
                    act.wait_ge(hl_done, JT * b)
                if n == 0 and later(b, 0, 1):
                    act.wait_ge(zl_done[0], b)
                for k in range(KC):
                    m = act.activation(z[n][:, k, :], ps[:, banks + k, :], ACT.Identity,
                                       bias=mod[:, 2 * shift + k, bass.ds(b, 1)], scale=mod[:, 2 * scale + k, bass.ds(b, 1)])
                m.then_inc(z_done[n], 1)

            def evacuate_y(b, g):
                act.wait_ge(pv_done, STEPS * b + TT * g + TT)
                if g >= 2:
                    act.wait_ge(y_written[g % 2], 32 * b + 16)
                elif later(b, 0, 1):
                    act.wait_ge(yn_done, b)
                act.activation(ysb[:, g % 2, :], ps[:, 4 + g % 2, :], ACT.Copy).then_inc(y_evac, 1)
                act.wait_ge(y_evac, NG * b + g + 1)
                act.dma_start(y_scr[G * g:G * (g + 1)].rearrange("h r s -> (h r) s"), ysb[:, g % 2, :]).then_inc(y_written[g % 2], 16)

            def step(i, par):
                if runs(i, 0):
                    act.wait_ge(parts_written, 64 * (i + 2) if runs(i, 1) else 64 * NB)
                    for s in range(STEPS):
                        for p in range(2):
                            act.wait_ge(st_done, 32 * i + 2 * s + p + 1)
                            if s >= 2:
                                act.wait_ge(pv_done, STEPS * i + s - 1)
                            elif later(i, 0, 1):
                                act.wait_ge(pv_done, STEPS * i)
                            act.activation(prob[:, s % 2, 2 * p:2 * p + 2, :], ps[:, 2 * p:2 * p + 2, :], ACT.Exp,
                                           scale=1.0 / DH).then_inc(exp_done, 1)
                        if s >= 5 and s % TT == 1:
                            evacuate_y(i, s // TT - 1)
                    evacuate_y(i, NG - 1)
                if runs(i, 2):
                    modulate(0, i + 2, 2, SH1, SC1)
                if runs(i, -1):
                    modulate(1, i - 1, 0, SH2, SC2)
                if runs(i, 0):
                    for n in range(2):
                        act.wait_ge(y_written[n], 32 * i + 32)
                    act.wait_ge(xg_done, i + 1)
                    for k in range(KC):
                        act.dma_start(yc[:, k, :], y_scr[8 * k:8 * k + 8, 0:DH, :]).then_inc(yc_loaded, 16)
                    act.dma_start(den, y_scr[:, DH, :]).then_inc(yc_loaded, 16)
                if runs(i, 2):
                    b = i + 2
                    for n in range(2):
                        act.wait_ge(v_done, 2 * b + n + 1)
                        act.activation(vaug[par][:, 2 * n:2 * n + 2, :, 0:DH],
                                       ps[:, n, :].rearrange("p (t h d) -> p t h d", t=2, d=DH), ACT.Copy).then_inc(vaug_done, 1)
                if runs(i, 0):
                    act.wait_ge(rec_done, i + 1)
                    act.dma_start(r_scr[:], rec).then_inc(r_written, 16)
                    act.wait_ge(r_written, 16 * i + 16)
                    for k in range(KC):
                        act.dma_start(rb[:, k, :], r_scr[8 * k:8 * k + 8].unsqueeze(1).broadcast_to([8, DH, S])).then_inc(rb_loaded, 16)
                if runs(i, -1):
                    b = i - 1
                    for j in range(JT):
                        act.wait_ge(w1_done, JT * b + j + 1)
                        if j >= HB:
                            act.wait_ge(hl_done, JT * b + j - HB + 1)
                        else:
                            act.wait_ge(zl_done[1], i)
                        act.activation(hb[:, j % HB, :], ps[:, 4 + j % 4, :], ACT.Gelu, bias=b1_t[:, j:j + 1]).then_inc(gelu_done, 1)

            schedule(step, act)

        @block.tensor
        def _(pe):
            def three(out_, ah, al, bh, bl, start, stop=True):
                for n, (a, b) in enumerate(((ah, bh), (ah, bl), (al, bh))):
                    m = pe.matmul(out_, a, b, start=start and n == 0, stop=stop and n == 2, skip_group_check=True)
                return m

            pe.wait_ge(ident_set, 2)
            pe.wait_ge(c6_loaded, 64)
            for k in range(KC):
                m = pe.transpose(ps[:, 0, k * NB:(k + 1) * NB], stage[0:NB, 1, k * P:(k + 1) * P], ident[0:NB, 0:NB])
            m.then_inc(prep_pe, 1)
            pe.wait_ge(prep_dve, 3)
            wc = [vaug[0][:].rearrange("p t h d -> p (t h d)"), qst[0][:].rearrange("p h s -> p (h s)").bitcast(F32)]
            for n in range(3):
                for k in range(KC):
                    m = pe.matmul(ps[0:NB, 1 + n, :], z[0][:, 1, k * NB:(k + 1) * NB], wc[k][:, n * 512:(n + 1) * 512],
                                  start=k == 0, stop=k == KC - 1)
            m.then_inc(prep_pe, 1)
            pe.wait_ge(prep_dve, 4)
            for n in range(12):
                m = pe.transpose(ps[:, 4, n * NB:(n + 1) * NB], stage[0:NB, 1, 256 + n * P:256 + (n + 1) * P], ident[0:NB, 0:NB])
            pe.wait_ge(w_loaded, 12 * 16)
            nb = 3 * KC + JT
            m = pe.transpose(ps[:, 4, 96:96 + nb], stage[0:nb, 1, 1792:1920], ident[0:nb, 0:nb])
            m.then_inc(prep_pe, 1)
            pe.wait_ge(prep_dve, 7)
            pe.wait_ge(const_set, 8)

            def transposes(n, b, bank):
                pe.wait_ge(xn_done[n], b + 1)
                for k in range(KC):
                    for t in range(TT):
                        m = pe.transpose(ps[:, bank + k, t * P:(t + 1) * P], xn[n][:, t, k * P:(k + 1) * P], ident[:])
                m.then_inc(tp_done[n], 1)

            def scores(b, par, n):
                h, t = n // TT, n % TT
                if n >= 2:
                    pe.wait_ge(max_done, 64 * b + n - 1)
                pe.matmul(ps[:, 6 + n % 2, :], qst[par][0:MROW, h, t * P:(t + 1) * P], kst[par][0:MROW, h, :],
                          start=True, stop=True).then_inc(s_done, 1)

            def pv(b, par, s):
                g, kt = s // TT, s % TT
                pe.wait_ge(exp_done, 32 * b + 2 * s + 2)
                if kt == 0:
                    if g >= 2:
                        pe.wait_ge(y_evac, NG * b + g - 1)
                    elif later(b, 0, 1):
                        pe.wait_ge(x1_gated, b)
                for q in range(G):
                    m = pe.matmul(ps[32 * q:32 * q + 32, 4 + g % 2, :], vaug[par][:, kt, G * g + q, :], prob[:, s % 2, q, :],
                                  start=kt == 0, stop=kt == TT - 1, skip_group_check=True)
                m.then_inc(pv_done, 1)

            def step(i, par):
                has_b, has_c, has_a, has_mlp = runs(i, 1), runs(i, 0), runs(i, 2), runs(i, -1)
                if has_b:
                    pe.wait_ge(stack_loaded, 192 * (i + 2))
                    if later(i, 0, 2):
                        pe.wait_ge(gelu_done, JT * (i - 1))
                    pe.wait_ge(rest_done, 4 * (i + 2))
                if has_c:
                    pe.wait_ge(m_loaded, 32 * (i + 1))
                    pe.wait_ge(vaug_done, 2 * (i + 2) if runs(i, 1) else 2 * NB)
                    if later(i, 0, 2):
                        pe.wait_ge(o_gated, i - 1)
                    for s in range(STEPS):
                        g, kt = s // TT, s % TT
                        for p in range(2):
                            if s:
                                pe.wait_ge(exp_done, 32 * i + 2 * s - 1 + p)
                            for q in (2 * p, 2 * p + 1):
                                m = pe.matmul(ps[:, q, :], kst[par][0:KROWS, G * g + q, kt * P:(kt + 1) * P],
                                              qst[par][0:KROWS, G * g + q, :], start=True, stop=True)
                            m.then_inc(st_done, 1)
                            if has_b:
                                scores(i + 1, 1 - par, 4 * s + 2 * p)
                                scores(i + 1, 1 - par, 4 * s + 2 * p + 1)
                        if s:
                            pv(i, par, s - 1)
                    pv(i, par, STEPS - 1)
                elif has_b:
                    for n in range(NH * TT):
                        scores(i + 1, 1 - par, n)
                if has_b:
                    pe.wait_ge(max_done, 64 * (i + 2))
                    for t in range(TT):
                        m = pe.transpose(ps[0:NH, 6, t * P:(t + 1) * P], mx[:, t, :], ident[:])
                    m.then_inc(mt_done, 1)
                if has_c:
                    pe.wait_ge(exp_done, 32 * (i + 1))
                if has_a:
                    if later(i, 2, 1) and not has_c:
                        pe.wait_ge(vaug_done, 2 * (i + 2))
                    transposes(0, i + 2, 2)
                if has_mlp:
                    transposes(1, i - 1, 0)
                if has_a:
                    b = i + 2
                    if has_c:
                        pe.wait_ge(y_evac, NG * (i + 1))
                    if has_b:
                        pe.wait_ge(mrow_done, 2 * (i + 2))
                    pe.wait_ge(zh_done[0], b + 1)
                    pe.wait_ge(zl_done[0], b + 1)
                    for j in range(4):
                        w, m_ = j // 2, j % 2
                        for k in range(KC):
                            f = slice(m_ * P, (m_ + 1) * P)
                            m = three(ps[:, 4 + j, :], wqkvo[0][:, w, k, f], wqkvo[1][:, w, k, f],
                                      zh[0][:, k, :], zl[0][:, k, :], k == 0, k == KC - 1)
                        m.then_inc(qk_done, 1)
                    if has_mlp:
                        pe.wait_ge(z_done[1], i)
                    for t in range(TT):
                        for k in range(KC):
                            f = slice(t * P, (t + 1) * P)
                            m = three(ps[:, t // 2, (t % 2) * H:(t % 2 + 1) * H], zh[0][:, k, f], zl[0][:, k, f],
                                      wqkvo[0][:, 2, k, :], wqkvo[1][:, 2, k, :], k == 0 and t % 2 == 0)
                        if t % 2:
                            m.then_inc(v_done, 1)
                if has_mlp:
                    b = i - 1
                    pe.wait_ge(zh_done[1], i)
                    pe.wait_ge(zl_done[1], i)

                    def up(j):
                        if j >= 4:
                            pe.wait_ge(gelu_done, JT * b + j - 3)
                        elif j == 0:
                            if has_a:
                                pe.wait_ge(rest_done, 4 * (i + 3))
                            else:
                                pe.wait_ge(y_evac, NG * (i + 1) if has_c else NG * NB)
                                pe.wait_ge(mrow_done, 2 * (i + 2) if has_b else 2 * NB)
                        for k in range(KC):
                            f = slice(j * P, (j + 1) * P)
                            m = three(ps[:, 4 + j % 4, :], w1[0][:, k, f], w1[1][:, k, f], zh[1][:, k, :], zl[1][:, k, :],
                                      k == 0, k == KC - 1)
                        m.then_inc(w1_done, 1)

                    def down(j):
                        pe.wait_ge(hl_done, JT * b + j + 1)
                        if j == 0:
                            pe.wait_ge(z_done[0], i + 3 if has_a else NB)
                            pe.wait_ge(vaug_done, 2 * (i + 3) if has_a else 2 * NB)
                        for t in range(TT):
                            f = slice(t * P, (t + 1) * P)
                            m = three(ps[:, t, 0:H], hh[:, j % HR, f], hl[:, j % HR, f], w2[0][:, j, :], w2[1][:, j, :],
                                      j == 0, j == JT - 1)
                        m.then_inc(w2_done, 1)

                    for j in range(3):
                        up(j)
                    for j in range(JT):
                        down(j)
                        if j + 3 < JT:
                            up(j + 3)
                if has_c:
                    pe.wait_ge(yh_done, i + 1)
                    pe.wait_ge(yl_done, i + 1)
                    if has_mlp:
                        pe.wait_ge(gelu_done, JT * i)
                    elif has_a:
                        pe.wait_ge(rest_done, 4 * (i + 3))
                    for t in range(TT):
                        f = slice(t * P, (t + 1) * P)
                        for k in range(KC):
                            m = three(ps[:, 4 + t // 2, (t % 2) * H:(t % 2 + 1) * H], yh[:, k, f], yl[:, k, f],
                                      wqkvo[0][:, 3, k, :], wqkvo[1][:, 3, k, :], k == 0 and t % 2 == 0)
                        if t % 2:
                            m.then_inc(wo_done, 1)

            schedule(step, pe)

        @block.vector
        def _(dve):
            dve.wait_ge(prep_act, 1)
            e = z[0][:, 0, 0:KC * NB]
            dve.tensor_scalar(e, e, 1.0, None, ALU.add).then_inc(prep_dve, 1)
            dve.wait_ge(prep_dve, 1)
            dve.reciprocal(z[0][:, 0, 64:64 + KC * NB], e).then_inc(prep_dve, 1)
            dve.wait_ge(prep_dve, 2)
            dve.tensor_tensor(z[0][:, 1, 0:KC * NB], ps[:, 0, 0:KC * NB], z[0][:, 0, 64:64 + KC * NB], ALU.mult).then_inc(prep_dve, 1)
            dve.wait_ge(prep_pe, 2)
            c6 = stage[0:NB, 1, 256:256 + 6 * H]
            dve.tensor_tensor(c6, ps[0:NB, 1:4, :].rearrange("p n f -> p (n f)"), c6, ALU.add).then_inc(prep_dve, 1)
            dve.wait_ge(w_loaded, 12 * 16)
            dve.tensor_copy(wqkvo[0][:].rearrange("p n c f -> p (n c f)"), stage[:, 0, :]).then_inc(w_split, 1)
            kf = kst[0][:].rearrange("p h s -> p (h s)").bitcast(F32)
            dve.tensor_copy(w1[0][:].rearrange("p c f -> p (c f)"), kf[:, 0:2048]).then_inc(w_split, 1)
            dve.tensor_copy(w2[0][:].rearrange("p c f -> p (c f)"), kf[:, 2048:4096]).then_inc(w_split, 1)
            dve.wait_ge(prep_pe, 3)
            dve.tensor_copy(mod[:].rearrange("p n b -> p (n b)"), ps[:, 4, 0:12 * NB]).then_inc(prep_dve, 1)
            dve.wait_ge(prep_dve, 5)
            for n in (SC1, SC2):
                m = dve.tensor_scalar(mod[:, 2 * n:2 * n + 2, :], mod[:, 2 * n:2 * n + 2, :], 1.0, None, ALU.add)
            m.then_inc(prep_dve, 1)
            dve.tensor_copy(bias_t[:], ps[:, 4, 96:96 + 3 * KC + JT]).then_inc(prep_dve, 1)
            dve.wait_ge(prep_dve, 7)

            def statistics(n, b, src):
                if later(b, 0, 1):
                    dve.wait_ge(xn_done[n], b)
                if n == 1:
                    dve.wait_ge(x1_done, b + 1)
                for t in range(TT):
                    m = dve.bn_stats(stats[n][:, t, :], src[:, t, :])
                m.then_inc(stat_done[n], 1)
                dve.wait_ge(stat_done[n], 3 * b + 1)
                dve.memset(vare[n][:], EPS)
                for t in range(TT):
                    m = dve.bn_aggr(mv[n][:, t, :], stats[n][:, t, :])
                m.then_inc(stat_done[n], 1)
                dve.wait_ge(stat_done[n], 3 * b + 2)
                dve.tensor_tensor(vare[n][:], mv[n][:, :, 1], vare[n][:], ALU.add).then_inc(stat_done[n], 1)

            def normalise(n, b, src):
                dve.wait_ge(rstd_done[n], b + 1)
                if n == 1 and later(b, 0, 1):
                    dve.wait_ge(out_written, 16 * b)
                dve.wait_ge(stat_done[n], 3 * b + 3)
                for t in range(TT):
                    m = dve.tensor_scalar(xn[n][:, t, :], src[:, t, :], mv[n][:, t, 0:1], rstd[n][:, t:t + 1],
                                          ALU.subtract, ALU.mult)
                m.then_inc(xn_done[n], 1)

            def row_max(b, n):
                dve.wait_ge(s_done, 64 * b + n + 1)
                h, t = n // TT, n % TT
                dve.tensor_reduce(mx[:, t, h:h + 1], ps[:, 6 + n % 2, :], AXX, ALU.max).then_inc(max_done, 1)

            def z_hi(n, b):
                dve.wait_ge(z_done[n], b + 1)
                dve.tensor_copy(zh[n][:], z[n][:]).then_inc(zh_done[n], 1)

            def step(i, par):
                has_b, has_c, has_a, has_mlp = runs(i, 1), runs(i, 0), runs(i, 2), runs(i, -1)
                if has_mlp:
                    statistics(1, i - 1, x1)
                for n in range(NH * TT):
                    if n == 8 and has_mlp:
                        normalise(1, i - 1, x1)
                    if n == 16 and has_a:
                        dve.wait_ge(xa_loaded, 16 * (i + 3))
                        statistics(0, i + 2, xa)
                    if n == 32 and has_a:
                        normalise(0, i + 2, xa)
                    if has_b:
                        if n == 0 and later(i, 1, 1):
                            dve.wait_ge(mt_done, i + 1)
                        row_max(i + 1, n)
                if has_b:
                    dve.wait_ge(mt_done, i + 2)
                    if later(i, 1, 1):
                        dve.wait_ge(m_loaded, 32 * (i + 1))
                    dve.tensor_copy(mrow[:, 0, :], ps[0:NH, 6, :]).then_inc(mrow_done, 1)
                    dve.wait_ge(mrow_done, 2 * (i + 1) + 1)
                    dve.tensor_tensor(mrow[:, 1, :], ps[0:NH, 6, :], mrow[:, 0, :], ALU.subtract).then_inc(mrow_done, 1)
                if has_a:
                    z_hi(0, i + 2)
                if has_mlp:
                    z_hi(1, i - 1)
                if has_a:
                    b = i + 2
                    if later(i, 2, 1):
                        dve.wait_ge(parts_written, 64 * b)
                    for j in range(4):
                        dve.wait_ge(qk_done, 4 * b + j + 1)
                        bias = bqk[:, j // 2, j % 2:j % 2 + 1]
                        dve.tensor_scalar(parts[:, j, 0, :], ps[:, 4 + j, :], bias, None, ALU.add).then_inc(part_h, 1)
                        dve.wait_ge(part_h, 4 * b + j + 1)
                        if j >= 2:
                            dve.wait_ge(part_l, 4 * b + j - 1)
                        dve.scalar_tensor_tensor(out=rest[:, j % 2, :], in0=ps[:, 4 + j, :], scalar=bias, in1=parts[:, j, 0, :],
                                                 op0=ALU.add, op1=ALU.subtract).then_inc(rest_done, 1)
                        dve.wait_ge(rest_done, 4 * b + j + 1)
                        dve.tensor_copy(parts[:, j, 1, :], rest[:, j % 2, :]).then_inc(part_m, 1)
                def denominators():
                    dve.wait_ge(yc_loaded, 48 * (i + 1))
                    dve.reciprocal(rec, den).then_inc(rec_done, 1)

                def y_norm():
                    dve.wait_ge(v_done, 2 * (i + 3) if has_a else 2 * NB)
                    dve.wait_ge(rb_loaded, 32 * (i + 1))
                    dve.tensor_tensor(yc[:], yc[:], rb[:], ALU.mult).then_inc(yn_done, 1)
                    dve.wait_ge(yn_done, i + 1)
                    for k in range(KC):
                        m = dve.tensor_scalar(yh[:, k, :], yc[:, k, :], bv_t[:, k:k + 1], None, ALU.add)
                    m.then_inc(yh_done, 1)
                    dve.wait_ge(yh_done, i + 1)
                    for k in range(KC):
                        m = dve.scalar_tensor_tensor(out=yl[:, k, :], in0=yc[:, k, :], scalar=bv_t[:, k:k + 1],
                                                     in1=yh[:, k, :].bitcast(F32), op0=ALU.add, op1=ALU.subtract)
                    m.then_inc(yl_done, 1)

                if has_c:
                    if later(i, 0, 1):
                        dve.wait_ge(r_written, 16 * i)
                    denominators()
                if has_mlp:
                    b = i - 1
                    for j in range(JT):
                        dve.wait_ge(gelu_done, JT * b + j + 1)
                        if j >= HR:
                            dve.wait_ge(w2_done, JT * b + j - HR + 1)
                        elif later(i, -1, 1):
                            dve.wait_ge(w2_done, JT * b)
                        dve.tensor_copy(hh[:, j % HR, :], hb[:, j % HB, :]).then_inc(hh_done, 1)
                        if j == 4 and has_c:
                            y_norm()
                    dve.wait_ge(w2_done, JT * i)
                    dve.tensor_tensor(osb[:], ps[:, 0:TT, 0:H], gm[:].unsqueeze(1).broadcast_to([P, TT, H]), ALU.mult).then_inc(o_gated, 1)
                    dve.wait_ge(o_gated, i)
                    dve.wait_ge(x1g_done, i)
                    dve.tensor_tensor(osb[:], osb[:], x1[:], ALU.add).then_inc(o_done, 1)
                elif has_c:
                    y_norm()
                if has_c:
                    dve.wait_ge(wo_done, 2 * (i + 1))
                    dve.wait_ge(xg_done, i + 1)
                    if later(i, 0, 1):
                        dve.wait_ge(o_done, i)
                    dve.tensor_tensor(x1[:], ps[:, 4:6, :].rearrange("p n (t f) -> p (n t) f", t=2),
                                      ga[:].unsqueeze(1).broadcast_to([P, TT, H]), ALU.mult).then_inc(x1_gated, 1)
                    dve.wait_ge(x1_gated, i + 1)
                    dve.tensor_tensor(x1[:], x1[:], xd[:], ALU.add).then_inc(x1_done, 1)

            schedule(step, dve)


_INS = ["x", "cond_1024"] + ["L0_cond_" + n for n in ("Wc", "bc", "Wq", "bq", "Wk", "bk", "Wv", "bv", "Wo", "bo", "W1", "b1", "W2", "b2")]


def kernel(**inputs):
    import numpy as _np
    import concourse.bacc as _bacc
    from concourse import mybir as _mybir
    from concourse.bass_utils import run_bass_kernel_spmd as _run

    nc = _bacc.Bacc("TRN2", target_bir_lowering=False, num_devices=1)
    arrays, args = {}, []
    for name in _INS:
        a = _np.ascontiguousarray(inputs[name])
        arrays[f"in_{name}_dram"] = a
        args.append(nc.dram_tensor(f"in_{name}_dram", a.shape, _mybir.dt.from_np(a.dtype), kind="ExternalInput").ap())
    args.append(nc.dram_tensor("out_0_dram", (NB, S, H), _mybir.dt.float32, kind="ExternalOutput").ap())
    args.append(nc.dram_tensor("c6_scratch", (NB, 6 * H), _mybir.dt.float32).ap())
    args.append(nc.dram_tensor("parts_scratch", (2, 3, H, S), _mybir.dt.bfloat16).ap())
    args.append(nc.dram_tensor("y_scratch", (NH, 2 * DH, S), _mybir.dt.float32).ap())
    args.append(nc.dram_tensor("r_scratch", (NH, S), _mybir.dt.float32).ap())
    dit_block(nc, *args)
    r = _run(nc, [arrays], core_ids=[0])
    return r.results[0]["out_0_dram"]
```

```python
from contextlib import ExitStack

import concourse.bass as bass
from concourse import mybir

F32 = mybir.dt.float32
F32R = mybir.dt.float32r
BF16 = mybir.dt.bfloat16
ALU = mybir.AluOpType
ACT = mybir.ActivationFunctionType
AXX = mybir.AxisListType.X

NB, S, H = 8, 512, 256
NH, DH = 16, 16
MLP = 4 * H
P = 128
KC = H // P
TT = S // P
JT = MLP // P
QPARTS = (0, 0, 1, 1, 0, 2)
KPARTS = (0, 1, 0, 1, 2, 0)
NSLOT = len(QPARTS)
MROW = NSLOT * DH
KROWS = MROW + 2
G = 4
NG = NH // G
STEPS = NG * TT
EPS = 1e-5
QK_BANKS = (4, 5, 2, 3)
C_BLOCKS = (1, 1) + (3,) * (STEPS - 2)
TURN_BLOCKS, QK_BLOCKS, V_BLOCKS = (1, 1), (0, 1, 0, 1), (0, 1, 0, 1)
UP_BLOCKS, DOWN_BLOCKS = (1, 1, 1), (2, 2, 2, 2, 2, 1, 0, 0)
assert sum(map(sum, (C_BLOCKS, TURN_BLOCKS, QK_BLOCKS, V_BLOCKS, UP_BLOCKS, DOWN_BLOCKS))) == NH * TT
HB, HR = 2, 3
SH1, SC1, G1, SH2, SC2, G2 = range(6)


def dit_block(nc, x, c, Wc, bc, Wq, bq, Wk, bk, Wv, bv, Wo, bo, W1, b1, W2, b2, out,
              c6_scr, parts_scr, y_scr, r_scr):
    with ExitStack() as ctx:
        def sb(name, shape, dt=F32):
            return ctx.enter_context(nc.sbuf_tensor(name, shape, dt))

        def sem(name):
            return ctx.enter_context(nc.semaphore(name))

        ps = ctx.enter_context(nc.psum_tensor("ps", [P, 8, 512], F32))

        wqkvo = [sb(f"wqkvo_{n}", [P, 4, KC, H], F32R) for n in ("hi", "lo")]
        w1 = [sb(f"w1_{n}", [P, KC, MLP], F32R) for n in ("hi", "lo")]
        w2 = [sb(f"w2_{n}", [P, JT, H], F32R) for n in ("hi", "lo")]
        bo_b = sb("bo_b", [P, H])
        b2_b = sb("b2_b", [P, H])
        bias_t = sb("bias_t", [P, 3 * KC + JT])
        bqk = bias_t[:, 0:2 * KC].rearrange("p (n c) -> p n c", n=2)
        bv_t = bias_t[:, 2 * KC:3 * KC]
        b1_t = bias_t[:, 3 * KC:]
        ident = sb("ident", [P, P])
        mhalf = sb("mhalf", [P, TT])
        warm = sb("warm", [P, 2])
        mod = sb("mod", [P, 12, NB])
        xa = sb("xa", [P, TT, H])
        xn = [xa, sb("xn2", [P, TT, H])]
        stats = [sb(f"stats{n}", [P, TT, 6]) for n in (1, 2)]
        mv = [sb(f"mv{n}", [P, TT, 2]) for n in (1, 2)]
        vare = [sb(f"vare{n}", [P, TT]) for n in (1, 2)]
        rstd = [sb(f"rstd{n}", [P, TT]) for n in (1, 2)]
        z1 = sb("z", [P, KC, S])
        z = [z1, z1]
        zh = [sb(f"zh{n}", [P, KC, S], F32R) for n in (1, 2)]
        zl = [sb(f"zl{n}", [P, KC, S], F32R) for n in (1, 2)]
        qst = [sb(f"qst{n}", [P, NH, S], BF16) for n in (0, 1)]
        kst = [sb(f"kst{n}", [P, NH, S], BF16) for n in (0, 1)]
        stage = qst[1][:].rearrange("p h s -> p (h s)").bitcast(F32).rearrange("p (n f) -> p n f", n=2)
        mlp_stage = kst[1][:].rearrange("p h s -> p (h s)").bitcast(F32)
        vaug = [sb(f"vaug{n}", [P, TT, NH, 2 * DH]) for n in (0, 1)]
        wc_half = [vaug[0][:].rearrange("p t h d -> p (t h d)")[:, 0:6 * H],
                   qst[0][:].rearrange("p h s -> p (h s)").bitcast(F32)[:, 0:6 * H]]
        mx = sb("mx", [P, TT, NH])
        mrow = sb("mrow", [NH, 2, S], BF16)
        prob = sb("prob", [P, 2, G, S])
        prob_flat = prob[:].rearrange("p n g s -> p (n g s)")
        parts = prob_flat[:, 0:6 * S].bitcast(BF16).rearrange("p (j n s) -> p j n s", j=4, n=3)
        rest = prob_flat[:, 6 * S:8 * S].rearrange("p (n s) -> p n s", n=2)
        yc = sb("yc", [P, KC, S])
        rb = sb("rb", [P, KC, S])
        den = rb[:, 0, 0:NH * S // P]
        rec = rb[:, 1, 0:NH * S // P]
        ysb = rb
        yh, yl = zh[0], zl[0]
        ga = sb("ga", [P, H])
        gm = sb("gm", [P, H])
        gbias = yc[:, 0, 0:H]
        xd = sb("xd", [P, TT, H])
        x1 = sb("x1", [P, TT, H])
        hb = z1
        hh = sb("hh", [P, HR, S], F32R)
        hl = sb("hl", [P, HR, S], F32R)
        osb = xn[1]

        c_loaded, wc_loaded, bc_loaded, bias_loaded = sem("c_loaded"), sem("wc_loaded"), sem("bc_loaded"), sem("bias_loaded")
        wqkvo_loaded, wmlp_loaded, w_split = sem("wqkvo_loaded"), sem("wmlp_loaded"), sem("w_split")
        c6_written, warm_set = sem("c6_written"), sem("warm_set")
        const_set, ident_set, prep_dve, prep_pe, prep_act = (
            sem("const_set"), sem("ident_set"), sem("prep_dve"), sem("prep_pe"), sem("prep_act"))
        xa_loaded = sem("xa_loaded")
        xd_loaded = sem("xd_loaded")
        ga_loaded = sem("ga_loaded")
        gm_loaded = sem("gm_loaded")
        stat_done = [sem(f"stat_done{n}") for n in (1, 2)]
        rstd_done = [sem(f"rstd_done{n}") for n in (1, 2)]
        xn_done = [sem(f"xn_done{n}") for n in (1, 2)]
        tp_done = [sem(f"tp_done{n}") for n in (1, 2)]
        z_done = [sem(f"z_done{n}") for n in (1, 2)]
        zh_done = [sem(f"zh_done{n}") for n in (1, 2)]
        zl_done = [sem(f"zl_done{n}") for n in (1, 2)]
        qk_done = sem("qk_done")
        part_h = sem("part_h")
        rest_done = sem("rest_done")
        part_m = sem("part_m")
        part_l = sem("part_l")
        parts_written = [sem(f"parts_written_{n}") for n in "qk"]
        stack_loaded = sem("stack_loaded")
        v_done = sem("v_done")
        vaug_done = sem("vaug_done")
        s_done = sem("s_done")
        max_done = sem("max_done")
        mt_done = sem("mt_done")
        mrow_done = sem("mrow_done")
        m_loaded = sem("m_loaded")
        st_done = sem("st_done")
        exp_done = sem("exp_done")
        pv_done = sem("pv_done")
        y_evac = sem("y_evac")
        y_written = [sem(f"y_written{n}") for n in (0, 1)]
        yc_loaded = sem("yc_loaded")
        rec_done = sem("rec_done")
        r_written = sem("r_written")
        rb_loaded = sem("rb_loaded")
        yn_done = sem("yn_done")
        yh_done = sem("yh_done")
        yl_done = sem("yl_done")
        wo_done = sem("wo_done")
        gbo_done = sem("gbo_done")
        xg_done = sem("xg_done")
        x1_gated = sem("x1_gated")
        x1_done = sem("x1_done")
        gb2_done = sem("gb2_done")
        x1g_done = sem("x1g_done")
        w1_done = sem("w1_done")
        gelu_done = sem("gelu_done")
        hh_done = sem("hh_done")
        hl_done = sem("hl_done")
        w2_done = sem("w2_done")
        o_gated = sem("o_gated")
        o_done = sem("o_done")
        out_written = sem("out_written")

        def schedule(step, engine):
            for i in (-2, -1, 0, 1):
                step(i, i % 2)
            with engine.Fori(2, 5, 2) as i:
                step(i, 0)
                step(i + 1, 1)
            for i in (6, 7, 8):
                step(i, i % 2)

        def runs(i, lag):
            return not isinstance(i, int) or 0 <= i + lag < NB

        def later(i, lag, n):
            return not isinstance(i, int) or i + lag >= n

        def early(i):
            return isinstance(i, int) and i < 0

        block = ctx.enter_context(nc.Block())

        @block.sync
        def _(sp):
            sp.dma_start(stage[0:NB, 1, 0:H], c).then_inc(c_loaded, 16)
            for k in range(KC):
                sp.dma_start(wc_half[k], Wc[k * P:(k + 1) * P, :]).then_inc(wc_loaded, 16)
            sp.dma_start(xa[:], x[0].rearrange("(t p) f -> p t f", p=P)).then_inc(xa_loaded, 16)
            sp.dma_start(stage[0:NB, 1, 256:256 + 6 * H], bc.rearrange("(o f) -> o f", o=1).broadcast_to([NB, 6 * H]))\
                .then_inc(bc_loaded, 16)
            for n, w in enumerate((Wq, Wk, Wv, Wo)):
                sp.dma_start(stage[:, 0, n * 512:(n + 1) * 512].rearrange("p (c f) -> p c f", c=KC),
                             w.rearrange("(c p) f -> p c f", p=P)).then_inc(wqkvo_loaded, 16)
            at = 0
            for b, rows in ((bq, KC), (bk, KC), (bv, KC), (b1, JT)):
                sp.dma_start(stage[at:at + rows, 1, 1792:1920], b.rearrange("(c p) -> c p", p=P)).then_inc(bias_loaded, 16)
                at += rows
            sp.dma_start(mlp_stage[:, 0:2048].rearrange("p (c f) -> p c f", c=KC), W1.rearrange("(c p) f -> p c f", p=P))\
                .then_inc(wmlp_loaded, 16)
            sp.dma_start(mlp_stage[:, 2048:4096].rearrange("p (c f) -> p c f", c=JT), W2.rearrange("(c p) f -> p c f", p=P))\
                .then_inc(wmlp_loaded, 16)
            for d, b in ((bo_b, bo), (b2_b, b2)):
                sp.dma_start(d[:], b.rearrange("(o f) -> o f", o=1).broadcast_to([P, H])).then_inc(wmlp_loaded, 16)
            sp.wait_ge(prep_dve, 4)
            sp.dma_start(c6_scr[:], stage[0:NB, 1, 256:256 + 6 * H]).then_inc(c6_written, 16)

            def step(i, par):
                if runs(i, 2) and later(i, 2, 1) and not early(i) or early(i) and not later(i, 2, 1):
                    b = i + 3 if early(i) else i + 2
                    sp.wait_ge(tp_done[0], b)
                    sp.dma_start(xa[:], x[bass.ds(b, 1)].rearrange("o (t p) f -> p (o t) f", p=P)).then_inc(xa_loaded, 16)
                if runs(i, 0):
                    if later(i, 0, 1):
                        sp.wait_ge(x1_done, i)
                    sp.dma_start(xd[:], x[bass.ds(i, 1)].rearrange("o (t p) f -> p (o t) f", p=P)).then_inc(xd_loaded, 16)
                    sp.dma_start(ga[:], c6_scr[bass.ds(i, 1), G1 * H:(G1 + 1) * H].broadcast_to([P, H])).then_inc(ga_loaded, 16)
                if runs(i, -1):
                    if later(i, -1, 1):
                        sp.wait_ge(o_gated, i - 1)
                    sp.dma_start(gm[:], c6_scr[bass.ds(i - 1, 1), G2 * H:(G2 + 1) * H].broadcast_to([P, H])).then_inc(gm_loaded, 16)
                if runs(i, 0):
                    for g in range(NG):
                        sp.wait_ge(y_evac, NG * i + g + 1)
                        sp.dma_start(y_scr[G * g:G * (g + 1)].rearrange("h r s -> (h r) s"), ysb[:, g % 2, :]).then_inc(y_written[g % 2], 16)
                    for n in range(2):
                        sp.wait_ge(y_written[n], 32 * i + 32)
                    sp.dma_start(den, y_scr[:, DH, :].rearrange("h (a s) -> h a s", s=NH * S // P)).then_inc(yc_loaded, 16)
                    sp.wait_ge(xg_done, i + 1)
                    for k in range(KC):
                        sp.dma_start(yc[:, k, :], y_scr[8 * k:8 * k + 8, 0:DH, :]).then_inc(yc_loaded, 16)

                def write_parts(b, j):
                    sp.wait_ge(part_l, 4 * b + j + 1)
                    m = j % 2
                    sp.dma_start(parts_scr[j // 2, :, m * P:(m + 1) * P, :].rearrange("n p s -> p n s"),
                                 parts[:, j, :, :]).then_inc(parts_written[j // 2], 16)

                def load_stack(b, w):
                    sp.wait_ge(parts_written[w], 32 * b + 32)
                    for slot in range(NSLOT):
                        stk, which = (qst, QPARTS) if w == 0 else (kst, KPARTS)
                        sp.dma_start(stk[par][slot * DH:(slot + 1) * DH, :, :],
                                     parts_scr[w, which[slot]].rearrange("(h d) s -> d h s", d=DH)).then_inc(stack_loaded, 16)

                if early(i) and later(i, 2, 1):
                    sp.wait_ge(c6_written, 16)
                    sp.wait_ge(prep_pe, 4)
                    sp.wait_ge(w_split, 4)
                    sp.wait_ge(const_set, 6)
                if runs(i, 2):
                    write_parts(i + 2, 0)
                    write_parts(i + 2, 1)
                    if early(i):
                        load_stack(i + 2, 0)
                if runs(i, 0):
                    sp.wait_ge(rec_done, i + 1)
                    sp.dma_start(r_scr.rearrange("h (a s) -> (h a) s", s=NH * S // P), rec).then_inc(r_written, 16)
                if runs(i, 2):
                    write_parts(i + 2, 2)
                    write_parts(i + 2, 3)
                if runs(i, 0):
                    sp.wait_ge(r_written, 16 * i + 16)
                    for k in range(KC):
                        sp.dma_start(rb[:, k, :], r_scr[8 * k:8 * k + 8].unsqueeze(1).broadcast_to([8, DH, S])).then_inc(rb_loaded, 16)
                if runs(i, 2):
                    if not early(i):
                        load_stack(i + 2, 0)
                    load_stack(i + 2, 1)
                if runs(i, 1):
                    b = i + 1
                    sp.wait_ge(mrow_done, 2 * b + 2)
                    for n in range(2):
                        sp.dma_start(qst[1 - par][MROW + n:MROW + n + 1, :, :],
                                     mrow[:, n, :]).then_inc(m_loaded, 16)
                if runs(i, -1):
                    sp.wait_ge(o_done, i)
                    sp.dma_start(out[bass.ds(i - 1, 1)].rearrange("o (t p) f -> p (o t) f", p=P), osb[:]).then_inc(out_written, 16)

            schedule(step, sp)
            sp.wait_ge(out_written, 16 * NB)

        @block.gpsimd
        def _(pool):
            pool.memset(ident[:], 0.0).then_inc(ident_set, 1)
            pool.wait_ge(ident_set, 1)
            pool.affine_select(out=ident[:], in_=ident[:], compare_op=ALU.not_equal, fill=1.0, base=0,
                               pattern=[[-1, P]], channel_multiplier=1).then_inc(ident_set, 1)
            pool.memset(warm[:], 0.0).then_inc(warm_set, 1)
            pool.memset(mhalf[:], -0.5).then_inc(const_set, 1)
            pool.wait_ge(const_set, 1)
            pool.memset(kst[0][MROW:KROWS, :, :], -1.0).then_inc(const_set, 1)
            pool.wait_ge(const_set, 2)
            pool.memset(vaug[1][:, :, :, DH:], 1.0).then_inc(const_set, 1)
            pool.wait_ge(const_set, 3)

            def mlp_weights():
                pool.wait_ge(w_split, 4)
                pool.tensor_tensor(w1[1][:].rearrange("p c f -> p (c f)"), mlp_stage[:, 0:2048],
                                   w1[0][:].rearrange("p c f -> p (c f)").bitcast(F32), ALU.subtract).then_inc(const_set, 1)
                pool.tensor_tensor(w2[1][:].rearrange("p c f -> p (c f)"), mlp_stage[:, 2048:4096],
                                   w2[0][:].rearrange("p c f -> p (c f)").bitcast(F32), ALU.subtract).then_inc(const_set, 1)
                pool.wait_ge(const_set, 6)
                pool.memset(kst[1][MROW:KROWS, :, :], -1.0).then_inc(const_set, 1)

            def norm(n, b):
                pool.wait_ge(stat_done[n], 3 * b + 3)
                pool.tensor_tensor(rstd[n][:], vare[n][:], mhalf[:], ALU.pow).then_inc(rstd_done[n], 1)

            def z_lo(n, b):
                pool.wait_ge(zh_done[n], 2 * b + 2)
                pool.tensor_tensor(zl[n][:], z[n][:], zh[n][:].bitcast(F32), ALU.subtract).then_inc(zl_done[n], 1)

            def step(i, par):
                if runs(i, -1):
                    norm(1, i - 1)
                if runs(i, 2):
                    norm(0, i + 2)
                if early(i) and not later(i, 2, 1):
                    pool.wait_ge(prep_pe, 2)
                    pool.memset(vaug[0][:, :, :, DH:], 1.0).then_inc(const_set, 1)
                if runs(i, -1):
                    pool.wait_ge(gm_loaded, 16 * i)
                    pool.wait_ge(yh_done, i)
                    pool.wait_ge(yl_done, i)
                    pool.tensor_tensor(gbias, gm[:], b2_b[:], ALU.mult).then_inc(gb2_done, 1)
                    pool.wait_ge(gb2_done, i)
                    pool.wait_ge(xn_done[1], i)
                    pool.tensor_tensor(x1[:], x1[:], gbias.unsqueeze(1).broadcast_to([P, TT, H]), ALU.add).then_inc(x1g_done, 1)
                if runs(i, 0):
                    pool.wait_ge(ga_loaded, 16 * i + 16)
                    if later(i, 0, 1):
                        pool.wait_ge(x1g_done, i)
                    pool.tensor_tensor(gbias, ga[:], bo_b[:], ALU.mult).then_inc(gbo_done, 1)
                    pool.wait_ge(gbo_done, i + 1)
                    pool.wait_ge(xd_loaded, 16 * i + 16)
                    pool.tensor_tensor(xd[:], xd[:], gbias.unsqueeze(1).broadcast_to([P, TT, H]), ALU.add).then_inc(xg_done, 1)
                if runs(i, 2):
                    b = i + 2
                    for j in range(4):
                        if j == 1 and runs(i, -1):
                            z_lo(1, i - 1)
                        pool.wait_ge(part_m, 4 * b + j + 1)
                        pool.tensor_tensor(parts[:, j, 2, :], rest[:, j % 2, :], parts[:, j, 1, :], ALU.subtract).then_inc(part_l, 1)
                    if early(i) and later(i, 2, 1):
                        mlp_weights()
                elif runs(i, -1):
                    z_lo(1, i - 1)
                if runs(i, -1):
                    b = i - 1
                    for j in range(JT):
                        pool.wait_ge(hh_done, JT * b + j + 1)
                        pool.tensor_tensor(hl[:, j % HR, :], hb[:, j % HB, :], hh[:, j % HR, :].bitcast(F32), ALU.subtract).then_inc(hl_done, 1)

            schedule(step, pool)

        @block.scalar
        def _(act):
            act.wait_ge(warm_set, 1)
            act.wait_ge(prep_pe, 1)
            act.activation(z[0][:, 0, 0:KC * NB], ps[:, 0, 0:KC * NB], ACT.Exp, scale=-1.0).then_inc(prep_act, 1)

            def load_table(func):
                act.activation(warm[:, 1:2], warm[:, 0:1], func)

            def modulate(n, b, banks, shift, scale):
                act.wait_ge(tp_done[n], b + 1)
                if n == 1 and later(b, 3, 3) and (not isinstance(b, int) or b + 3 < NB):
                    act.wait_ge(zl_done[0], b + 4)
                if n == 0 and later(b, -4, 0):
                    act.wait_ge(hl_done, JT * (b - 3))
                if n == 1 and later(b, -1, 0):
                    act.wait_ge(hl_done, JT * b)
                if n == 0 and later(b, 0, 1):
                    act.wait_ge(zl_done[0], b)
                for k in range(KC):
                    act.activation(z[n][:, k, :], ps[:, banks + k, :], ACT.Identity, bias=mod[:, 2 * shift + k, bass.ds(b, 1)],
                                   scale=mod[:, 2 * scale + k, bass.ds(b, 1)]).then_inc(z_done[n], 1)

            def evacuate_y(b, g):
                act.wait_ge(pv_done, STEPS * b + TT * g + TT)
                if g >= 2:
                    act.wait_ge(y_written[g % 2], 32 * b + 16)
                elif later(b, 0, 1):
                    act.wait_ge(yn_done, b)
                act.activation(ysb[:, g % 2, :], ps[:, 4 + g % 2, :], ACT.Copy).then_inc(y_evac, 1)

            def step(i, par):
                if runs(i, 0):
                    for w in range(2):
                        act.wait_ge(parts_written[w], 32 * (i + 2) if runs(i, 1) else 32 * NB)
                    for s in range(STEPS):
                        for p in range(2):
                            act.wait_ge(st_done, 32 * i + 2 * s + p + 1)
                            if s >= 2:
                                act.wait_ge(pv_done, STEPS * i + s - 1)
                            elif later(i, 0, 1):
                                act.wait_ge(pv_done, STEPS * i)
                            act.activation(prob[:, s % 2, 2 * p:2 * p + 2, :], ps[:, 2 * p:2 * p + 2, :], ACT.Exp,
                                           scale=1.0 / DH).then_inc(exp_done, 1)
                        if s >= 5 and s % TT == 1:
                            evacuate_y(i, s // TT - 1)
                if runs(i, 2):
                    if not later(i, 2, 1):
                        act.wait_ge(prep_dve, 7)
                    modulate(0, i + 2, 2, SH1, SC1)
                if runs(i, 0):
                    evacuate_y(i, NG - 1)
                if runs(i, -1):
                    modulate(1, i - 1, 0, SH2, SC2)
                if runs(i, 2):
                    b = i + 2
                    for j in range(4):
                        act.wait_ge(qk_done, 4 * b + j + 1)
                        if j % 2 == 0 and later(i, 2, 1) and not runs(i, 0):
                            act.wait_ge(parts_written[j // 2], 32 * b)
                        act.activation(parts[:, j, 0, :], ps[:, QK_BANKS[j], :], ACT.Identity,
                                       bias=bqk[:, j // 2, j % 2:j % 2 + 1]).then_inc(part_h, 1)
                    for n in range(2):
                        act.wait_ge(v_done, 2 * b + n + 1)
                        act.activation(vaug[par][:, 2 * n:2 * n + 2, :, 0:DH],
                                       ps[:, 4 + n, :].rearrange("p (t h d) -> p t h d", t=2, d=DH), ACT.Copy).then_inc(vaug_done, 1)
                if runs(i, -1):
                    b = i - 1
                    load_table(ACT.Gelu)
                    for j in range(JT):
                        act.wait_ge(w1_done, JT * b + j + 1)
                        if j >= HB:
                            act.wait_ge(hl_done, JT * b + j - HB + 1)
                        else:
                            act.wait_ge(zl_done[1], i)
                        act.activation(hb[:, j % HB, :], ps[:, 4 + j % 2, :], ACT.Gelu, bias=b1_t[:, j:j + 1]).then_inc(gelu_done, 1)
                    if runs(i, 1):
                        load_table(ACT.Exp)

            schedule(step, act)

        @block.tensor
        def _(pe):
            def three(out_, ah, al, bh, bl, start, stop=True):
                for n, (a, b) in enumerate(((ah, bh), (ah, bl), (al, bh))):
                    m = pe.matmul(out_, a, b, start=start and n == 0, stop=stop and n == 2, skip_group_check=True)
                return m

            pe.wait_ge(ident_set, 2)
            pe.wait_ge(c_loaded, 16)
            for k in range(KC):
                m = pe.transpose(ps[:, 0, k * NB:(k + 1) * NB], stage[0:NB, 1, k * P:(k + 1) * P], ident[0:NB, 0:NB])
            m.then_inc(prep_pe, 1)
            pe.wait_ge(prep_dve, 3)
            pe.wait_ge(wc_loaded, 16 * KC)
            for n in range(3):
                for k in range(KC):
                    m = pe.matmul(ps[0:NB, 1 + n, :], z[0][:, 1, k * NB:(k + 1) * NB], wc_half[k][:, n * 512:(n + 1) * 512],
                                  start=k == 0, stop=k == KC - 1)
            m.then_inc(prep_pe, 1)
            pe.wait_ge(prep_dve, 4)
            for n in range(12):
                m = pe.transpose(ps[:, 4, n * NB:(n + 1) * NB], stage[0:NB, 1, 256 + n * P:256 + (n + 1) * P], ident[0:NB, 0:NB])
            m.then_inc(prep_pe, 1)
            pe.wait_ge(bias_loaded, 64)
            nb = 3 * KC + JT
            pe.transpose(ps[:, 5, 0:nb], stage[0:nb, 1, 1792:1920], ident[0:nb, 0:nb]).then_inc(prep_pe, 1)

            def transposes(n, b, bank):
                pe.wait_ge(xn_done[n], b + 1)
                for k in range(KC):
                    for t in range(TT):
                        m = pe.transpose(ps[:, bank + k, t * P:(t + 1) * P], xn[n][:, t, k * P:(k + 1) * P], ident[:])
                m.then_inc(tp_done[n], 1)

            block_at = [0]

            def scores(i, par, blocks, banks=(6, 7)):
                for _ in range(blocks if runs(i, 1) else 0):
                    n = block_at[0]
                    block_at[0] = (n + 1) % (NH * TT)
                    h, t = n // TT, n % TT
                    if n >= len(banks):
                        pe.wait_ge(max_done, 64 * (i + 1) + n - len(banks) + 1)
                    elif n == 0:
                        pe.wait_ge(stack_loaded, 192 * (i + 2))
                        if later(i, 1, 1):
                            pe.wait_ge(mrow_done, 2 * (i + 1))
                    pe.matmul(ps[:, banks[n % len(banks)], :], qst[1 - par][0:MROW, h, t * P:(t + 1) * P], kst[1 - par][0:MROW, h, :],
                              start=True, stop=True).then_inc(s_done, 1)

            def turn_maxima(i):
                if runs(i, 1):
                    pe.wait_ge(max_done, 64 * (i + 2))
                    for t in range(TT):
                        m = pe.transpose(ps[0:NH, 6, t * P:(t + 1) * P], mx[:, t, :], ident[:])
                    m.then_inc(mt_done, 1)

            def pv(b, par, s):
                g, kt = s // TT, s % TT
                pe.wait_ge(exp_done, 32 * b + 2 * s + 2)
                if kt == 0:
                    if g >= 2:
                        pe.wait_ge(y_evac, NG * b + g - 1)
                    elif later(b, 0, 1):
                        pe.wait_ge(x1_gated, b)
                for q in range(G):
                    m = pe.matmul(ps[32 * q:32 * q + 32, 4 + g % 2, :], vaug[par][:, kt, G * g + q, :], prob[:, s % 2, q, :],
                                  start=kt == 0, stop=kt == TT - 1, skip_group_check=True)
                m.then_inc(pv_done, 1)

            def step(i, par):
                has_b, has_c, has_a, has_mlp = runs(i, 1), runs(i, 0), runs(i, 2), runs(i, -1)
                others = (lambda n: 0) if early(i) else (lambda n: n)
                if has_c:
                    if not later(i, 0, 1):
                        pe.wait_ge(const_set, 7)
                    pe.wait_ge(m_loaded, 32 * (i + 1))
                    pe.wait_ge(vaug_done, 2 * (i + 2) if has_b else 2 * NB)
                    pe.wait_ge(part_l, 4 * (i + 2) if has_b else 4 * NB)
                    if later(i, 0, 2):
                        pe.wait_ge(o_gated, i - 1)
                    for s in range(STEPS):
                        g, kt = s // TT, s % TT
                        for p in range(2):
                            if s:
                                pe.wait_ge(exp_done, 32 * i + 2 * s - 1 + p)
                            for q in (2 * p, 2 * p + 1):
                                m = pe.matmul(ps[:, q, :], kst[par][0:KROWS, G * g + q, kt * P:(kt + 1) * P],
                                              qst[par][0:KROWS, G * g + q, :], start=True, stop=True)
                            m.then_inc(st_done, 1)
                            scores(i, par, min(1, C_BLOCKS[s] - p))
                        if s:
                            pv(i, par, s - 1)
                        scores(i, par, C_BLOCKS[s] - 2)
                    pe.wait_ge(exp_done, 32 * (i + 1))
                if has_a:
                    if later(i, 2, 1) and not has_c:
                        pe.wait_ge(rest_done, 4 * (i + 2))
                    transposes(0, i + 2, 2)
                if has_c:
                    pv(i, par, STEPS - 1)
                scores(i, par, others(TURN_BLOCKS[0]))
                if has_mlp:
                    transposes(1, i - 1, 0)
                scores(i, par, others(TURN_BLOCKS[1]))
                if has_a:
                    b = i + 2
                    if not later(i, 2, 1):
                        pe.wait_ge(w_split, 2)
                        pe.wait_ge(prep_dve, 7)
                    for w in range(2):
                        for m in range(2):
                            if w == 0 and has_c:
                                pe.wait_ge(y_evac, NG * (i + 1) + m - 1)
                            for k in range(KC):
                                if w == 0 and m == 0:
                                    pe.wait_ge(zh_done[0], 2 * b + k + 1)
                                for n in range(2):
                                    pe.matmul(ps[:, QK_BANKS[2 * w + m], :], wqkvo[n][:, w, k, m * P:(m + 1) * P], zh[0][:, k, :],
                                              start=k == 0 and n == 0, stop=False)
                        pe.wait_ge(zl_done[0], b + 1)
                        for m in range(2):
                            for k in range(KC):
                                last = pe.matmul(ps[:, QK_BANKS[2 * w + m], :], wqkvo[0][:, w, k, m * P:(m + 1) * P], zl[0][:, k, :],
                                                 start=False, stop=k == KC - 1)
                            last.then_inc(qk_done, 1)
                            scores(i, par, others(QK_BLOCKS[2 * w + m]))
                    for t in range(TT):
                        if t % 2 == 0:
                            pe.wait_ge(rest_done, 4 * b + t // 2 + 1)
                        for k in range(KC):
                            f = slice(t * P, (t + 1) * P)
                            m = three(ps[:, 4 + t // 2, (t % 2) * H:(t % 2 + 1) * H], zh[0][:, k, f], zl[0][:, k, f],
                                      wqkvo[0][:, 2, k, :], wqkvo[1][:, 2, k, :], k == 0 and t % 2 == 0)
                        if t % 2:
                            m.then_inc(v_done, 1)
                        scores(i, par, others(V_BLOCKS[t]))
                else:
                    scores(i, par, others(sum(QK_BLOCKS + V_BLOCKS)))
                if has_mlp:
                    b = i - 1

                    def up(j):
                        if j >= 2:
                            pe.wait_ge(gelu_done, JT * b + j - 1)
                        elif j == 0:
                            pe.wait_ge(zh_done[1], 2 * i)
                            pe.wait_ge(zl_done[1], i)
                            if has_a:
                                pe.wait_ge(vaug_done, 2 * (i + 3))
                            else:
                                pe.wait_ge(y_evac, NG * (i + 1) if has_c else NG * NB)
                        for k in range(KC):
                            f = slice(j * P, (j + 1) * P)
                            m = three(ps[:, 4 + j % 2, :], w1[0][:, k, f], w1[1][:, k, f], zh[1][:, k, :], zl[1][:, k, :],
                                      k == 0, k == KC - 1)
                        m.then_inc(w1_done, 1)

                    def down(j):
                        pe.wait_ge(hl_done, JT * b + j + 1)
                        if j == 0:
                            pe.wait_ge(rest_done, 4 * (i + 3) if has_a else 4 * NB)
                        for t in range(TT):
                            f = slice(t * P, (t + 1) * P)
                            m = three(ps[:, t, 0:H], hh[:, j % HR, f], hl[:, j % HR, f], w2[0][:, j, :], w2[1][:, j, :],
                                      j == 0, j == JT - 1)
                        m.then_inc(w2_done, 1)

                    for j in range(3):
                        up(j)
                        scores(i, par, UP_BLOCKS[j])
                    for j in range(JT):
                        down(j)
                        scores(i, par, DOWN_BLOCKS[j])
                        if j == 5:
                            turn_maxima(i)
                        if j + 3 < JT:
                            up(j + 3)
                elif early(i):
                    scores(i, par, NH * TT, (6, 7, 0, 1))
                    turn_maxima(i)
                else:
                    scores(i, par, sum(UP_BLOCKS + DOWN_BLOCKS))
                    turn_maxima(i)
                if has_c:
                    pe.wait_ge(yh_done, i + 1)
                    pe.wait_ge(yl_done, i + 1)
                    if has_mlp:
                        pe.wait_ge(gelu_done, JT * i)
                    elif has_a:
                        pe.wait_ge(vaug_done, 2 * (i + 3))
                    for t in range(TT):
                        f = slice(t * P, (t + 1) * P)
                        for k in range(KC):
                            m = three(ps[:, 4 + t // 2, (t % 2) * H:(t % 2 + 1) * H], yh[:, k, f], yl[:, k, f],
                                      wqkvo[0][:, 3, k, :], wqkvo[1][:, 3, k, :], k == 0 and t % 2 == 0)
                        if t % 2:
                            m.then_inc(wo_done, 1)

            schedule(step, pe)

        @block.vector
        def _(dve):
            dve.wait_ge(prep_act, 1)
            e = z[0][:, 0, 0:KC * NB]
            dve.tensor_scalar(e, e, 1.0, None, ALU.add).then_inc(prep_dve, 1)
            dve.wait_ge(prep_dve, 1)
            dve.reciprocal(z[0][:, 0, 64:64 + KC * NB], e).then_inc(prep_dve, 1)
            dve.wait_ge(prep_dve, 2)
            dve.tensor_tensor(z[0][:, 1, 0:KC * NB], ps[:, 0, 0:KC * NB], z[0][:, 0, 64:64 + KC * NB], ALU.mult).then_inc(prep_dve, 1)
            def statistics(n, b, src, t):
                if t == 0:
                    if later(b, 0, 1):
                        dve.wait_ge(xn_done[n], b)
                    if n == 1:
                        dve.wait_ge(x1_done, b + 1)
                    else:
                        dve.wait_ge(xa_loaded, 16 * (b + 1))
                m = dve.bn_stats(stats[n][:, t, :], src[:, t, :])
                if t == TT - 1:
                    m.then_inc(stat_done[n], 1)

            def variance(n, b):
                dve.wait_ge(stat_done[n], 3 * b + 1)
                dve.memset(vare[n][:], EPS)
                for t in range(TT):
                    m = dve.bn_aggr(mv[n][:, t, :], stats[n][:, t, :])
                m.then_inc(stat_done[n], 1)
                dve.wait_ge(stat_done[n], 3 * b + 2)
                dve.tensor_tensor(vare[n][:], mv[n][:, :, 1], vare[n][:], ALU.add).then_inc(stat_done[n], 1)

            def normalise(n, b, src, t):
                if t == 0:
                    dve.wait_ge(rstd_done[n], b + 1)
                    if n == 1 and later(b, 0, 1):
                        dve.wait_ge(out_written, 16 * b)
                    dve.wait_ge(stat_done[n], 3 * b + 3)
                m = dve.tensor_scalar(xn[n][:, t, :], src[:, t, :], mv[n][:, t, 0:1], rstd[n][:, t:t + 1],
                                      ALU.subtract, ALU.mult)
                if t == TT - 1:
                    m.then_inc(xn_done[n], 1)

            def norm_piece(n, b, src, k):
                if k < TT:
                    statistics(n, b, src, k)
                elif k == TT:
                    variance(n, b)
                elif k > TT:
                    normalise(n, b, src, k - TT - 1)

            for t in range(TT):
                statistics(0, 0, xa, t)
            variance(0, 0)
            dve.wait_ge(prep_pe, 2)
            dve.wait_ge(bc_loaded, 16)
            c6 = stage[0:NB, 1, 256:256 + 6 * H]
            dve.tensor_tensor(c6, ps[0:NB, 1:4, :].rearrange("p n f -> p (n f)"), c6, ALU.add).then_inc(prep_dve, 1)
            for t in range(TT):
                normalise(0, 0, xa, t)
            dve.wait_ge(prep_pe, 3)
            dve.tensor_copy(mod[:].rearrange("p n b -> p (n b)"), ps[:, 4, 0:12 * NB]).then_inc(prep_dve, 1)
            dve.wait_ge(prep_dve, 5)
            for n in (SC1, SC2):
                m = dve.tensor_scalar(mod[:, 2 * n:2 * n + 2, :], mod[:, 2 * n:2 * n + 2, :], 1.0, None, ALU.add)
            m.then_inc(prep_dve, 1)
            dve.wait_ge(wqkvo_loaded, 64)
            dve.tensor_copy(wqkvo[0][:].rearrange("p n c f -> p (n c f)"), stage[:, 0, :]).then_inc(w_split, 1)
            dve.wait_ge(w_split, 1)
            dve.tensor_tensor(wqkvo[1][:].rearrange("p n c f -> p (n c f)"), stage[:, 0, :],
                              wqkvo[0][:].rearrange("p n c f -> p (n c f)").bitcast(F32), ALU.subtract).then_inc(w_split, 1)
            dve.wait_ge(prep_pe, 4)
            dve.tensor_copy(bias_t[:], ps[:, 5, 0:3 * KC + JT]).then_inc(prep_dve, 1)
            dve.wait_ge(prep_dve, 7)

            block_at = [0]

            def row_max(i, blocks, banks=(6, 7)):
                if not runs(i, 1):
                    return
                for _ in range(blocks):
                    n = block_at[0]
                    block_at[0] = (n + 1) % (NH * TT)
                    if n == 0 and later(i, 1, 1):
                        dve.wait_ge(mt_done, i + 1)
                    dve.wait_ge(s_done, 64 * (i + 1) + n + 1)
                    h, t = n // TT, n % TT
                    dve.tensor_reduce(mx[:, t, h:h + 1], ps[:, banks[n % len(banks)], :], AXX, ALU.max).then_inc(max_done, 1)

            def z_hi(n, b):
                for k in range(KC):
                    dve.wait_ge(z_done[n], 2 * b + k + 1)
                    dve.tensor_copy(zh[n][:, k, :], z[n][:, k, :]).then_inc(zh_done[n], 1)

            def step(i, par):
                has_b, has_c, has_a, has_mlp = runs(i, 1), runs(i, 0), runs(i, 2), runs(i, -1)
                others = (lambda n: 0) if early(i) else (lambda n: n)
                def maxima_rows():
                    if not has_b:
                        return
                    dve.wait_ge(mt_done, i + 2)
                    if later(i, 1, 1):
                        dve.wait_ge(m_loaded, 32 * (i + 1))
                    dve.tensor_copy(mrow[:, 0, :], ps[0:NH, 6, :]).then_inc(mrow_done, 1)
                    dve.wait_ge(mrow_done, 2 * (i + 1) + 1)
                    dve.tensor_tensor(mrow[:, 1, :], ps[0:NH, 6, :], mrow[:, 0, :], ALU.subtract).then_inc(mrow_done, 1)

                ln2 = {2: (0, 1), 3: (2, 3), 4: (4,), 7: (5, 6), 8: (7, 8)}
                ln1 = {5: (0, 1), 6: (2, 3), 9: (4,), 12: (5, 6), 13: (7, 8)}
                for s in range(STEPS):
                    for n in range(3):
                        if has_c:
                            row_max(i, min(1, max(0, C_BLOCKS[s] - n)))
                        if n < 2:
                            if has_mlp:
                                for k in ln2.get(s, ())[n:n + 1]:
                                    norm_piece(1, i - 1, x1, k)
                            if has_a and later(i, 2, 1):
                                for k in ln1.get(s, ())[n:n + 1]:
                                    norm_piece(0, i + 2, xa, k)
                row_max(i, others(TURN_BLOCKS[0]))
                if has_a:
                    z_hi(0, i + 2)
                    dve.wait_ge(zh_done[0], 2 * (i + 3))
                    dve.tensor_tensor(zl[0][:], z[0][:], zh[0][:].bitcast(F32), ALU.subtract).then_inc(zl_done[0], 1)
                row_max(i, others(TURN_BLOCKS[1]))
                if has_mlp:
                    z_hi(1, i - 1)

                def rest_of(b, j):
                    dve.wait_ge(part_h, 4 * b + j + 1)
                    if j >= 2:
                        dve.wait_ge(part_l, 4 * b + j - 1)
                    dve.scalar_tensor_tensor(out=rest[:, j % 2, :], in0=ps[:, QK_BANKS[j], :], scalar=bqk[:, j // 2, j % 2:j % 2 + 1],
                                             in1=parts[:, j, 0, :], op0=ALU.add, op1=ALU.subtract).then_inc(rest_done, 1)
                    dve.wait_ge(rest_done, 4 * b + j + 1)
                    dve.tensor_copy(parts[:, j, 1, :], rest[:, j % 2, :]).then_inc(part_m, 1)

                for j in range(4):
                    if j == 3:
                        row_max(i, others(QK_BLOCKS[3] + sum(V_BLOCKS[0:2])))
                    if has_a:
                        rest_of(i + 2, j)
                    if j == 1 and has_c:
                        dve.wait_ge(yc_loaded, 48 * (i + 1))
                        dve.reciprocal(rec, den).then_inc(rec_done, 1)
                    if j < 3:
                        row_max(i, others(QK_BLOCKS[j]))
                row_max(i, others(sum(V_BLOCKS[2:4])))
                if early(i) and later(i, 2, 1):
                    dve.wait_ge(wmlp_loaded, 64)
                    dve.tensor_copy(w1[0][:].rearrange("p c f -> p (c f)"), mlp_stage[:, 0:2048]).then_inc(w_split, 1)
                    dve.tensor_copy(w2[0][:].rearrange("p c f -> p (c f)"), mlp_stage[:, 2048:4096]).then_inc(w_split, 1)

                def y_norm(part):
                    if part == 0:
                        dve.wait_ge(rb_loaded, 32 * (i + 1))
                        dve.tensor_tensor(yc[:], yc[:], rb[:], ALU.mult).then_inc(yn_done, 1)
                    if part == 1:
                        dve.wait_ge(v_done, 2 * (i + 3) if has_a else 2 * NB)
                        dve.wait_ge(yn_done, i + 1)
                        for k in range(KC):
                            m = dve.tensor_scalar(yh[:, k, :], yc[:, k, :], bv_t[:, k:k + 1], None, ALU.add)
                        m.then_inc(yh_done, 1)
                    if part == 2:
                        dve.wait_ge(yh_done, i + 1)
                        for k in range(KC):
                            m = dve.scalar_tensor_tensor(out=yl[:, k, :], in0=yc[:, k, :], scalar=bv_t[:, k:k + 1],
                                                         in1=yh[:, k, :].bitcast(F32), op0=ALU.add, op1=ALU.subtract)
                        m.then_inc(yl_done, 1)

                if has_mlp:
                    b = i - 1
                    row_max(i, UP_BLOCKS[0])
                    for j in range(JT):
                        dve.wait_ge(gelu_done, JT * b + j + 1)
                        if j >= HR:
                            dve.wait_ge(w2_done, JT * b + j - HR + 1)
                        elif later(i, -1, 1):
                            dve.wait_ge(w2_done, JT * b)
                        dve.tensor_copy(hh[:, j % HR, :], hb[:, j % HB, :]).then_inc(hh_done, 1)
                        if j + 1 < len(UP_BLOCKS):
                            row_max(i, UP_BLOCKS[j + 1])
                        elif j >= 2:
                            row_max(i, DOWN_BLOCKS[j - 2])
                        if j == 7:
                            maxima_rows()
                        if j >= 5 and has_c:
                            y_norm(j - 5)
                    dve.wait_ge(w2_done, JT * i)
                    dve.tensor_tensor(osb[:], ps[:, 0:TT, 0:H], gm[:].unsqueeze(1).broadcast_to([P, TT, H]), ALU.mult).then_inc(o_gated, 1)
                    dve.wait_ge(o_gated, i)
                    dve.wait_ge(x1g_done, i)
                    dve.tensor_tensor(osb[:], osb[:], x1[:], ALU.add).then_inc(o_done, 1)
                else:
                    if early(i):
                        row_max(i, NH * TT, (6, 7, 0, 1))
                    else:
                        row_max(i, sum(UP_BLOCKS + DOWN_BLOCKS))
                    maxima_rows()
                    if has_c:
                        for part in range(3):
                            y_norm(part)
                if has_c:
                    dve.wait_ge(wo_done, 2 * (i + 1))
                    dve.wait_ge(xg_done, i + 1)
                    if later(i, 0, 1):
                        dve.wait_ge(o_done, i)
                    dve.tensor_tensor(x1[:], ps[:, 4:6, :].rearrange("p n (t f) -> p (n t) f", t=2),
                                      ga[:].unsqueeze(1).broadcast_to([P, TT, H]), ALU.mult).then_inc(x1_gated, 1)
                    dve.wait_ge(x1_gated, i + 1)
                    dve.tensor_tensor(x1[:], x1[:], xd[:], ALU.add).then_inc(x1_done, 1)

            schedule(step, dve)


_INS = ["x", "cond_1024"] + ["L0_cond_" + n for n in ("Wc", "bc", "Wq", "bq", "Wk", "bk", "Wv", "bv", "Wo", "bo", "W1", "b1", "W2", "b2")]


def kernel(**inputs):
    import numpy as _np
    import concourse.bacc as _bacc
    from concourse import mybir as _mybir
    from concourse.bass_utils import run_bass_kernel_spmd as _run

    nc = _bacc.Bacc("TRN2", target_bir_lowering=False, num_devices=1)
    arrays, args = {}, []
    for name in _INS:
        a = _np.ascontiguousarray(inputs[name])
        arrays[f"in_{name}_dram"] = a
        args.append(nc.dram_tensor(f"in_{name}_dram", a.shape, _mybir.dt.from_np(a.dtype), kind="ExternalInput").ap())
    args.append(nc.dram_tensor("out_0_dram", (NB, S, H), _mybir.dt.float32, kind="ExternalOutput").ap())
    args.append(nc.dram_tensor("c6_scratch", (NB, 6 * H), _mybir.dt.float32).ap())
    args.append(nc.dram_tensor("parts_scratch", (2, 3, H, S), _mybir.dt.bfloat16).ap())
    args.append(nc.dram_tensor("y_scratch", (NH, 2 * DH, S), _mybir.dt.float32).ap())
    args.append(nc.dram_tensor("r_scratch", (NH, S), _mybir.dt.float32).ap())
    dit_block(nc, *args)
    r = _run(nc, [arrays], core_ids=[0])
    return r.results[0]["out_0_dram"]
```

```python
from contextlib import ExitStack

import concourse.bass as bass
from concourse import mybir

F32 = mybir.dt.float32
F32R = mybir.dt.float32r
BF16 = mybir.dt.bfloat16
ALU = mybir.AluOpType
ACT = mybir.ActivationFunctionType
AXX = mybir.AxisListType.X

NB, S, H = 8, 512, 256
NH, DH = 16, 16
MLP = 4 * H
P = 128
KC = H // P
TT = S // P
JT = MLP // P
QPARTS = (0, 0, 1, 1, 0, 2)
KPARTS = (0, 1, 0, 1, 2, 0)
NSLOT = len(QPARTS)
MROW = NSLOT * DH
KROWS = MROW + 2
G = 4
NG = NH // G
STEPS = NG * TT
EPS = 1e-5
QK_BANKS = (4, 5, 2, 3)
C_BLOCKS = (1, 0) + (3,) * (STEPS - 4) + (4, 4)
TURN_BLOCKS, QK_BLOCKS, V_BLOCKS = (1, 1), (0, 1, 0, 1), (0, 1, 0, 1)
UP_BLOCKS, DOWN_BLOCKS = (1, 1, 1), (2, 2, 2, 2, 2, 0, 0, 0)
assert sum(map(sum, (C_BLOCKS, TURN_BLOCKS, QK_BLOCKS, V_BLOCKS, UP_BLOCKS, DOWN_BLOCKS))) == NH * TT
HALF, EXTRA = NH * TT // 2, 8
OLD_BLOCKS = (4,) * 6 + (0,) * (STEPS - 6)
NEW_BLOCKS = (0,) * 6 + (4,) * (STEPS - 6)
OLD_TURN = 5
assert HALF + EXTRA + sum(OLD_BLOCKS) == NH * TT and OLD_TURN < STEPS // 2
WO_AT, LN2_AT, TURN_AT = 2, 5, 5
HB, HR = 2, 3
SH1, SC1, G1, SH2, SC2, G2 = range(6)


def dit_block(nc, x, c, Wc, bc, Wq, bq, Wk, bk, Wv, bv, Wo, bo, W1, b1, W2, b2, out,
              c6_scr, parts_scr, y_scr, r_scr):
    with ExitStack() as ctx:
        def sb(name, shape, dt=F32):
            return ctx.enter_context(nc.sbuf_tensor(name, shape, dt))

        def sem(name):
            return ctx.enter_context(nc.semaphore(name))

        ps = ctx.enter_context(nc.psum_tensor("ps", [P, 8, 512], F32))

        wqkvo = [sb(f"wqkvo_{n}", [P, 4, KC, H], F32R) for n in ("hi", "lo")]
        w1 = [sb(f"w1_{n}", [P, KC, MLP], F32R) for n in ("hi", "lo")]
        w2 = [sb(f"w2_{n}", [P, JT, H], F32R) for n in ("hi", "lo")]
        bo_b = sb("bo_b", [P, H])
        b2_b = sb("b2_b", [P, H])
        bias_t = sb("bias_t", [P, 3 * KC + JT])
        bqk = bias_t[:, 0:2 * KC].rearrange("p (n c) -> p n c", n=2)
        bv_t = bias_t[:, 2 * KC:3 * KC]
        b1_t = bias_t[:, 3 * KC:]
        ident = sb("ident", [P, P])
        mhalf = sb("mhalf", [P, TT])
        warm = sb("warm", [P, 2])
        mod = sb("mod", [P, 12, NB])
        xa = sb("xa", [P, TT, H])
        xn = [xa, sb("xn2", [P, TT, H])]
        stats = [sb(f"stats{n}", [P, TT, 6]) for n in (1, 2)]
        mv = [sb(f"mv{n}", [P, TT, 2]) for n in (1, 2)]
        vare = [sb(f"vare{n}", [P, TT]) for n in (1, 2)]
        rstd = [sb(f"rstd{n}", [P, TT]) for n in (1, 2)]
        z1 = sb("z", [P, KC, S])
        z = [z1, z1]
        zh = [sb(f"zh{n}", [P, KC, S], F32R) for n in (1, 2)]
        zl = [sb(f"zl{n}", [P, KC, S], F32R) for n in (1, 2)]
        qst = [sb(f"qst{n}", [P, NH, S], BF16) for n in (0, 1)]
        kst = [sb(f"kst{n}", [P, NH, S], BF16) for n in (0, 1)]
        stage = qst[1][:].rearrange("p h s -> p (h s)").bitcast(F32).rearrange("p (n f) -> p n f", n=2)
        mlp_stage = kst[1][:].rearrange("p h s -> p (h s)").bitcast(F32)
        vaug = [sb(f"vaug{n}", [P, TT, NH, 2 * DH]) for n in (0, 1)]
        wc_half = [vaug[0][:].rearrange("p t h d -> p (t h d)")[:, 0:6 * H],
                   qst[0][:].rearrange("p h s -> p (h s)").bitcast(F32)[:, 0:6 * H]]
        mx = sb("mx", [P, TT, NH])
        mrow = sb("mrow", [NH, 2, S], BF16)
        prob = sb("prob", [P, 2, G, S])
        prob_flat = prob[:].rearrange("p n g s -> p (n g s)")
        parts = prob_flat[:, 0:6 * S].bitcast(BF16).rearrange("p (j n s) -> p j n s", j=4, n=3)
        rest = prob_flat[:, 6 * S:8 * S].rearrange("p (n s) -> p n s", n=2)
        yc = sb("yc", [P, KC, S])
        rb = sb("rb", [P, KC, S])
        den = rb[:, 0, 0:NH * S // P]
        rec = rb[:, 1, 0:NH * S // P]
        ysb = rb
        yh, yl = zh[0], zl[0]
        ga = sb("ga", [P, H])
        gm = sb("gm", [P, H])
        gbias = yc[:, 0, 0:H]
        xd = sb("xd", [P, TT, H])
        x1 = sb("x1", [P, TT, H])
        hb = z1
        hh = sb("hh", [P, HR, S], F32R)
        hl = sb("hl", [P, HR, S], F32R)
        osb = xn[1]

        c_loaded, wc_loaded, bc_loaded, bias_loaded = sem("c_loaded"), sem("wc_loaded"), sem("bc_loaded"), sem("bias_loaded")
        wqkvo_loaded, wmlp_loaded, w_split = sem("wqkvo_loaded"), sem("wmlp_loaded"), sem("w_split")
        c6_written, warm_set = sem("c6_written"), sem("warm_set")
        const_set, ident_set, prep_dve, prep_pe, prep_act = (
            sem("const_set"), sem("ident_set"), sem("prep_dve"), sem("prep_pe"), sem("prep_act"))
        xa_loaded = sem("xa_loaded")
        xd_loaded = sem("xd_loaded")
        ga_loaded = sem("ga_loaded")
        gm_loaded = sem("gm_loaded")
        stat_done = [sem(f"stat_done{n}") for n in (1, 2)]
        rstd_done = [sem(f"rstd_done{n}") for n in (1, 2)]
        xn_done = [sem(f"xn_done{n}") for n in (1, 2)]
        tp_done = [sem(f"tp_done{n}") for n in (1, 2)]
        z_done = [sem(f"z_done{n}") for n in (1, 2)]
        zh_done = [sem(f"zh_done{n}") for n in (1, 2)]
        zl_done = [sem(f"zl_done{n}") for n in (1, 2)]
        qk_done = sem("qk_done")
        part_h = sem("part_h")
        rest_done = sem("rest_done")
        part_m = sem("part_m")
        part_l = sem("part_l")
        parts_written = [sem(f"parts_written_{n}") for n in "qk"]
        stack_loaded = sem("stack_loaded")
        v_done = sem("v_done")
        vaug_done = sem("vaug_done")
        s_done = sem("s_done")
        max_done = sem("max_done")
        mt_done = sem("mt_done")
        mrow_done = sem("mrow_done")
        m_loaded = sem("m_loaded")
        half_turned, half_rows, half_loaded = sem("half_turned"), sem("half_rows"), sem("half_loaded")
        st_done = sem("st_done")
        exp_done = sem("exp_done")
        pv_done = sem("pv_done")
        y_evac = sem("y_evac")
        y_written = [sem(f"y_written{n}") for n in (0, 1)]
        den_loaded = sem("den_loaded")
        yc_loaded = sem("yc_loaded")
        rec_done = sem("rec_done")
        r_written = sem("r_written")
        rb_loaded = sem("rb_loaded")
        yn_done = sem("yn_done")
        yh_done = sem("yh_done")
        yl_done = sem("yl_done")
        wo_done = sem("wo_done")
        gbo_done = sem("gbo_done")
        xg_done = sem("xg_done")
        x1_gated = sem("x1_gated")
        x1_done = sem("x1_done")
        gb2_done = sem("gb2_done")
        x1g_done = sem("x1g_done")
        w1_done = sem("w1_done")
        gelu_done = sem("gelu_done")
        hh_done = sem("hh_done")
        hl_done = sem("hl_done")
        w2_done = sem("w2_done")
        o_gated = sem("o_gated")
        o_done = sem("o_done")
        out_written = sem("out_written")

        def schedule(step, engine):
            for i in (-2, -1, 0, 1):
                step(i, i % 2)
            with engine.Fori(2, 5, 2) as i:
                step(i, 0)
                step(i + 1, 1)
            for i in (6, 7, 8):
                step(i, i % 2)

        def runs(i, lag):
            return not isinstance(i, int) or 0 <= i + lag < NB

        def later(i, lag, n):
            return not isinstance(i, int) or i + lag >= n

        def final(b):
            return isinstance(b, int) and b == NB - 1

        def z_of(n, b):
            return rb if n == 1 and final(b) else z[n]

        def zh_of(n, b):
            return zh[0] if final(b) else zh[n]

        def zl_of(n, b):
            return zl[0] if final(b) else zl[n]

        def xn_of(n, b):
            return xd if n == 1 and final(b) else xn[n]

        def x1_of(b):
            return xa if final(b) else x1

        def c_blocks(i, s):
            return (OLD_BLOCKS[s], NEW_BLOCKS[s]) if isinstance(i, int) and i == 0 else (0, C_BLOCKS[s])

        def tail_blocks(i):
            new = NEW_BLOCKS if isinstance(i, int) and i == 0 else C_BLOCKS
            return NH * TT - sum(map(sum, (new, TURN_BLOCKS, QK_BLOCKS, V_BLOCKS)))

        def early(i):
            return isinstance(i, int) and i < 0

        block = ctx.enter_context(nc.Block())

        @block.sync
        def _(sp):
            sp.dma_start(stage[0:NB, 1, 0:H], c).then_inc(c_loaded, 16)
            for k in range(KC):
                sp.dma_start(wc_half[k], Wc[k * P:(k + 1) * P, :]).then_inc(wc_loaded, 16)
            sp.dma_start(xa[:], x[0].rearrange("(t p) f -> p t f", p=P)).then_inc(xa_loaded, 16)
            sp.dma_start(stage[0:NB, 1, 256:256 + 6 * H], bc.rearrange("(o f) -> o f", o=1).broadcast_to([NB, 6 * H]))\
                .then_inc(bc_loaded, 16)
            for n, w in enumerate((Wq, Wk, Wv, Wo)):
                sp.dma_start(stage[:, 0, n * 512:(n + 1) * 512].rearrange("p (c f) -> p c f", c=KC),
                             w.rearrange("(c p) f -> p c f", p=P)).then_inc(wqkvo_loaded, 16)
            at = 0
            for b, rows in ((bq, KC), (bk, KC), (bv, KC), (b1, JT)):
                sp.dma_start(stage[at:at + rows, 1, 1792:1920], b.rearrange("(c p) -> c p", p=P)).then_inc(bias_loaded, 16)
                at += rows
            sp.dma_start(mlp_stage[:, 0:2048].rearrange("p (c f) -> p c f", c=KC), W1.rearrange("(c p) f -> p c f", p=P))\
                .then_inc(wmlp_loaded, 16)
            sp.dma_start(mlp_stage[:, 2048:4096].rearrange("p (c f) -> p c f", c=JT), W2.rearrange("(c p) f -> p c f", p=P))\
                .then_inc(wmlp_loaded, 16)
            for d, b in ((bo_b, bo), (b2_b, b2)):
                sp.dma_start(d[:], b.rearrange("(o f) -> o f", o=1).broadcast_to([P, H])).then_inc(wmlp_loaded, 16)
            sp.wait_ge(prep_dve, 4)
            sp.dma_start(c6_scr[:], stage[0:NB, 1, 256:256 + 6 * H]).then_inc(c6_written, 16)

            def step(i, par):
                if runs(i, 2) and later(i, 2, 1) and not early(i) or early(i) and not later(i, 2, 1):
                    b = i + 3 if early(i) else i + 2
                    sp.wait_ge(tp_done[0], b)
                    sp.dma_start(xa[:], x[bass.ds(b, 1)].rearrange("o (t p) f -> p (o t) f", p=P)).then_inc(xa_loaded, 16)
                if runs(i, 0):
                    if later(i, 0, 1):
                        sp.wait_ge(x1_done, i)
                    sp.dma_start(xd[:], x[bass.ds(i, 1)].rearrange("o (t p) f -> p (o t) f", p=P)).then_inc(xd_loaded, 16)
                    sp.dma_start(ga[:], c6_scr[bass.ds(i, 1), G1 * H:(G1 + 1) * H].broadcast_to([P, H])).then_inc(ga_loaded, 16)
                if runs(i, -1):
                    if later(i, -1, 1):
                        sp.wait_ge(o_gated, i - 1)
                    sp.dma_start(gm[:], c6_scr[bass.ds(i - 1, 1), G2 * H:(G2 + 1) * H].broadcast_to([P, H])).then_inc(gm_loaded, 16)

                def load_maxima(stack, first, last, loaded):
                    for n in range(2):
                        sp.dma_start(stack[MROW + n:MROW + n + 1, first:last, :], mrow[0:last - first, n, :]).then_inc(loaded, 16)

                if runs(i, 0) and not later(i, 0, 1):
                    sp.wait_ge(mrow_done, 2)
                    load_maxima(qst[par], NH // 2, NH, m_loaded)
                if runs(i, 0):
                    for g in range(NG):
                        sp.wait_ge(y_evac, NG * i + g + 1)
                        sp.dma_start(y_scr[G * g:G * (g + 1)].rearrange("h r s -> (h r) s"), ysb[:, g % 2, :]).then_inc(y_written[g % 2], 16)
                    for n in range(2):
                        sp.wait_ge(y_written[n], 32 * i + 32)
                    sp.dma_start(den, y_scr[:, DH, :].rearrange("h (a s) -> h a s", s=NH * S // P)).then_inc(den_loaded, 16)
                    sp.wait_ge(xg_done, i + 1)
                    for k in range(KC):
                        sp.dma_start(yc[:, k, :], y_scr[8 * k:8 * k + 8, 0:DH, :]).then_inc(yc_loaded, 16)

                def write_parts(b, j):
                    sp.wait_ge(part_l, 4 * b + j + 1)
                    m = j % 2
                    sp.dma_start(parts_scr[j // 2, :, m * P:(m + 1) * P, :].rearrange("n p s -> p n s"),
                                 parts[:, j, :, :]).then_inc(parts_written[j // 2], 16)

                def load_stack(b, w):
                    sp.wait_ge(parts_written[w], 32 * b + 32)
                    for slot in range(NSLOT):
                        stk, which = (qst, QPARTS) if w == 0 else (kst, KPARTS)
                        sp.dma_start(stk[par][slot * DH:(slot + 1) * DH, :, :],
                                     parts_scr[w, which[slot]].rearrange("(h d) s -> d h s", d=DH)).then_inc(stack_loaded, 16)

                if early(i) and later(i, 2, 1):
                    sp.wait_ge(stack_loaded, 192)
                if runs(i, 2):
                    write_parts(i + 2, 0)
                    write_parts(i + 2, 1)
                if runs(i, 0):
                    sp.wait_ge(rec_done, i + 1)
                    sp.dma_start(r_scr.rearrange("h (a s) -> (h a) s", s=NH * S // P), rec).then_inc(r_written, 16)
                if runs(i, 2):
                    write_parts(i + 2, 2)
                    write_parts(i + 2, 3)
                if runs(i, 0):
                    sp.wait_ge(r_written, 16 * i + 16)
                    for k in range(KC):
                        sp.dma_start(rb[:, k, :], r_scr[8 * k:8 * k + 8].unsqueeze(1).broadcast_to([8, DH, S])).then_inc(rb_loaded, 16)
                if runs(i, 2):
                    if early(i) and later(i, 2, 1):
                        sp.wait_ge(c6_written, 16)
                        sp.wait_ge(prep_pe, 4)
                        sp.wait_ge(w_split, 2)
                    load_stack(i + 2, 0)
                    if early(i) and later(i, 2, 1):
                        sp.wait_ge(const_set, 6)
                    load_stack(i + 2, 1)
                if early(i) and runs(i, 1):
                    sp.wait_ge(half_rows, 2)
                    load_maxima(qst[1 - par], 0, NH // 2, half_loaded)
                elif runs(i, 1):
                    sp.wait_ge(mrow_done, 2 * i + 4)
                    load_maxima(qst[1 - par], 0, NH, m_loaded)
                if runs(i, -1):
                    sp.wait_ge(o_done, i)
                    sp.dma_start(out[bass.ds(i - 1, 1)].rearrange("o (t p) f -> p (o t) f", p=P), osb[:]).then_inc(out_written, 16)

            schedule(step, sp)
            sp.wait_ge(out_written, 16 * NB)

        @block.gpsimd
        def _(pool):
            pool.memset(ident[:], 0.0).then_inc(ident_set, 1)
            pool.wait_ge(ident_set, 1)
            pool.affine_select(out=ident[:], in_=ident[:], compare_op=ALU.not_equal, fill=1.0, base=0,
                               pattern=[[-1, P]], channel_multiplier=1).then_inc(ident_set, 1)
            pool.memset(warm[:], 0.0).then_inc(warm_set, 1)
            pool.memset(mhalf[:], -0.5).then_inc(const_set, 1)
            pool.wait_ge(const_set, 1)
            pool.memset(kst[0][MROW:KROWS, :, :], -1.0).then_inc(const_set, 1)
            pool.wait_ge(const_set, 2)
            pool.memset(vaug[1][:, :, :, DH:], 1.0).then_inc(const_set, 1)
            pool.wait_ge(const_set, 3)

            def mlp_weights():
                pool.wait_ge(w_split, 4)
                pool.tensor_tensor(w1[1][:].rearrange("p c f -> p (c f)"), mlp_stage[:, 0:2048],
                                   w1[0][:].rearrange("p c f -> p (c f)").bitcast(F32), ALU.subtract).then_inc(const_set, 1)
                pool.tensor_tensor(w2[1][:].rearrange("p c f -> p (c f)"), mlp_stage[:, 2048:4096],
                                   w2[0][:].rearrange("p c f -> p (c f)").bitcast(F32), ALU.subtract).then_inc(const_set, 1)
                pool.wait_ge(const_set, 6)
                pool.memset(kst[1][MROW:KROWS, :, :], -1.0).then_inc(const_set, 1)

            def norm(n, b):
                pool.wait_ge(stat_done[n], 3 * b + 3)
                pool.tensor_tensor(rstd[n][:], vare[n][:], mhalf[:], ALU.pow).then_inc(rstd_done[n], 1)

            def z_lo(n, b):
                pool.wait_ge(zh_done[n], 2 * b + 2)
                pool.tensor_tensor(zl[n][:], z[n][:], zh[n][:].bitcast(F32), ALU.subtract).then_inc(zl_done[n], 1)

            def step(i, par):
                if runs(i, -1) and not final(i - 1):
                    norm(1, i - 1)
                if runs(i, 2) and later(i, 2, 2):
                    norm(0, i + 2)
                if early(i) and not later(i, 2, 1):
                    norm(0, 0)
                    pool.wait_ge(prep_pe, 2)
                    pool.memset(vaug[0][:, :, :, DH:], 1.0).then_inc(const_set, 1)
                    norm(0, 1)

                def add_b2():
                    pool.wait_ge(gm_loaded, 16 * i)
                    pool.wait_ge(yh_done, i)
                    pool.wait_ge(yl_done, i)
                    pool.tensor_tensor(gbias, gm[:], b2_b[:], ALU.mult).then_inc(gb2_done, 1)
                    pool.wait_ge(gb2_done, i)
                    pool.wait_ge(xn_done[1], i)
                    pool.tensor_tensor(x1_of(i - 1)[:], x1_of(i - 1)[:], gbias.unsqueeze(1).broadcast_to([P, TT, H]),
                                       ALU.add).then_inc(x1g_done, 1)

                if runs(i, -1) and not final(i - 1):
                    add_b2()
                if runs(i, 0):
                    pool.wait_ge(ga_loaded, 16 * i + 16)
                    if later(i, 0, 1):
                        pool.wait_ge(x1g_done, i)
                    pool.tensor_tensor(gbias, ga[:], bo_b[:], ALU.mult).then_inc(gbo_done, 1)
                    pool.wait_ge(gbo_done, i + 1)
                    pool.wait_ge(xd_loaded, 16 * i + 16)
                    pool.tensor_tensor(xd[:], xd[:], gbias.unsqueeze(1).broadcast_to([P, TT, H]), ALU.add).then_inc(xg_done, 1)
                if runs(i, 2):
                    b = i + 2
                    for j in range(4):
                        if j == 2 and runs(i, -1):
                            z_lo(1, i - 1)
                        pool.wait_ge(part_m, 4 * b + j + 1)
                        pool.tensor_tensor(parts[:, j, 2, :], rest[:, j % 2, :], parts[:, j, 1, :], ALU.subtract).then_inc(part_l, 1)
                    if early(i) and later(i, 2, 1):
                        mlp_weights()
                if runs(i, -1):
                    b = i - 1
                    for j in range(JT):
                        pool.wait_ge(hh_done, JT * b + j + 1)
                        pool.tensor_tensor(hl[:, j % HR, :], hb[:, j % HB, :], hh[:, j % HR, :].bitcast(F32), ALU.subtract).then_inc(hl_done, 1)
                        if final(i) and j == LN2_AT:
                            norm(1, i)
                        if final(b) and j == JT // 2:
                            add_b2()

            schedule(step, pool)

        @block.scalar
        def _(act):
            act.wait_ge(warm_set, 1)
            act.wait_ge(prep_pe, 1)
            act.activation(z[0][:, 0, 0:KC * NB], ps[:, 0, 0:KC * NB], ACT.Exp, scale=-1.0).then_inc(prep_act, 1)

            def load_table(func):
                act.activation(warm[:, 1:2], warm[:, 0:1], func)

            def modulate(n, b, banks, shift, scale):
                act.wait_ge(tp_done[n], b + 1)
                if n == 1 and later(b, 3, 3) and (not isinstance(b, int) or b + 3 < NB):
                    act.wait_ge(zl_done[0], b + 4)
                if n == 0 and later(b, -4, 0):
                    act.wait_ge(hl_done, JT * (b - 3))
                if n == 1 and final(b):
                    act.wait_ge(yn_done, NB)
                elif n == 1 and later(b, -1, 0):
                    act.wait_ge(hl_done, JT * b)
                if n == 0 and later(b, 0, 1):
                    act.wait_ge(zl_done[0], b)
                for k in range(KC):
                    act.activation(z_of(n, b)[:, k, :], ps[:, banks + k, :], ACT.Identity, bias=mod[:, 2 * shift + k, bass.ds(b, 1)],
                                   scale=mod[:, 2 * scale + k, bass.ds(b, 1)]).then_inc(z_done[n], 1)

            def evacuate_y(b, g):
                act.wait_ge(pv_done, STEPS * b + TT * g + TT)
                if g >= 2:
                    act.wait_ge(y_written[g % 2], 32 * b + 16)
                elif later(b, 0, 1):
                    act.wait_ge(yn_done, b)
                act.activation(ysb[:, g % 2, :], ps[:, 4 + g % 2, :], ACT.Copy).then_inc(y_evac, 1)

            def step(i, par):
                if runs(i, 0):
                    for w in range(2):
                        act.wait_ge(parts_written[w], 32 * (i + 2) if runs(i, 1) else 32 * NB)
                    for s in range(STEPS):
                        for p in range(2):
                            act.wait_ge(st_done, 32 * i + 2 * s + p + 1)
                            if s >= 2:
                                act.wait_ge(pv_done, STEPS * i + s - 1)
                            elif later(i, 0, 1):
                                act.wait_ge(pv_done, STEPS * i)
                            act.activation(prob[:, s % 2, 2 * p:2 * p + 2, :], ps[:, 2 * p:2 * p + 2, :], ACT.Exp,
                                           scale=1.0 / DH).then_inc(exp_done, 1)
                        if s >= 5 and s % TT == 1:
                            evacuate_y(i, s // TT - 1)
                if runs(i, 2):
                    if not later(i, 2, 1):
                        act.wait_ge(prep_dve, 7)
                    modulate(0, i + 2, 2, SH1, SC1)
                if runs(i, 0):
                    evacuate_y(i, NG - 1)
                if runs(i, -1) and not final(i - 1):
                    modulate(1, i - 1, 0, SH2, SC2)
                if runs(i, 2):
                    b = i + 2
                    for j in range(4):
                        act.wait_ge(qk_done, 4 * b + j + 1)
                        if j % 2 == 0 and later(i, 2, 1) and not runs(i, 0):
                            act.wait_ge(parts_written[j // 2], 32 * b)
                        act.activation(parts[:, j, 0, :], ps[:, QK_BANKS[j], :], ACT.Identity,
                                       bias=bqk[:, j // 2, j % 2:j % 2 + 1]).then_inc(part_h, 1)
                    for n in range(2):
                        act.wait_ge(v_done, 2 * b + n + 1)
                        act.activation(vaug[par][:, 2 * n:2 * n + 2, :, 0:DH],
                                       ps[:, 4 + n, :].rearrange("p (t h d) -> p t h d", t=2, d=DH), ACT.Copy).then_inc(vaug_done, 1)
                if early(i) and not later(i, 2, 1):
                    act.wait_ge(wmlp_loaded, 64)
                    act.activation(w1[0][:].rearrange("p c f -> p (c f)"), mlp_stage[:, 0:2048], ACT.Copy).then_inc(w_split, 1)
                    act.activation(w2[0][:].rearrange("p c f -> p (c f)"), mlp_stage[:, 2048:4096], ACT.Copy).then_inc(w_split, 1)
                if runs(i, -1):
                    b = i - 1
                    if not final(b):
                        load_table(ACT.Gelu)
                    for j in range(JT):
                        act.wait_ge(w1_done, JT * b + j + 1)
                        if j >= HB or final(b):
                            act.wait_ge(hl_done, JT * b + j - HB + 1)
                        else:
                            act.wait_ge(zl_done[1], i)
                        act.activation(hb[:, j % HB, :], ps[:, 4 + j % 2, :], ACT.Gelu, bias=b1_t[:, j:j + 1]).then_inc(gelu_done, 1)
                    if runs(i, 1):
                        load_table(ACT.Exp)
                    if final(i):
                        modulate(1, i, 6, SH2, SC2)

            schedule(step, act)

        @block.tensor
        def _(pe):
            def three(out_, ah, al, bh, bl, start, stop=True):
                for n, (a, b) in enumerate(((ah, bh), (ah, bl), (al, bh))):
                    m = pe.matmul(out_, a, b, start=start and n == 0, stop=stop and n == 2, skip_group_check=True)
                return m

            pe.wait_ge(ident_set, 2)
            pe.wait_ge(c_loaded, 16)
            for k in range(KC):
                m = pe.transpose(ps[:, 0, k * NB:(k + 1) * NB], stage[0:NB, 1, k * P:(k + 1) * P], ident[0:NB, 0:NB])
            m.then_inc(prep_pe, 1)
            pe.wait_ge(prep_dve, 3)
            pe.wait_ge(wc_loaded, 16 * KC)
            for n in range(3):
                for k in range(KC):
                    m = pe.matmul(ps[0:NB, 1 + n, :], z[0][:, 1, k * NB:(k + 1) * NB], wc_half[k][:, n * 512:(n + 1) * 512],
                                  start=k == 0, stop=k == KC - 1)
            m.then_inc(prep_pe, 1)
            pe.wait_ge(prep_dve, 4)
            for n in range(12):
                m = pe.transpose(ps[:, 4, n * NB:(n + 1) * NB], stage[0:NB, 1, 256 + n * P:256 + (n + 1) * P], ident[0:NB, 0:NB])
            m.then_inc(prep_pe, 1)
            pe.wait_ge(bias_loaded, 64)
            nb = 3 * KC + JT
            pe.transpose(ps[:, 5, 0:nb], stage[0:nb, 1, 1792:1920], ident[0:nb, 0:nb]).then_inc(prep_pe, 1)

            def transposes(n, b, bank):
                pe.wait_ge(xn_done[n], b + 1)
                for k in range(KC):
                    for t in range(TT):
                        m = pe.transpose(ps[:, bank + k, t * P:(t + 1) * P], xn_of(n, b)[:, t, k * P:(k + 1) * P], ident[:])
                m.then_inc(tp_done[n], 1)

            block_at = [0]

            def scores(i, par, blocks, banks=(6, 7)):
                for _ in range(blocks if runs(i, 1) else 0):
                    n = block_at[0]
                    block_at[0] = (n + 1) % (NH * TT)
                    h, t = n // TT, n % TT
                    if n >= len(banks):
                        pe.wait_ge(max_done, 64 * (i + 1) + n - len(banks) + 1)
                    elif n == 0:
                        pe.wait_ge(stack_loaded, 192 * (i + 2))
                        if later(i, 1, 1):
                            pe.wait_ge(mrow_done, 2 * (i + 1))
                    pe.matmul(ps[:, banks[n % len(banks)], :], qst[1 - par][0:MROW, h, t * P:(t + 1) * P], kst[1 - par][0:MROW, h, :],
                              start=True, stop=True).then_inc(s_done, 1)

            def turn_maxima(i, first=0, last=NH, turned=mt_done, bank=6):
                if runs(i, 1):
                    pe.wait_ge(max_done, 64 * (i + 1) + TT * last)
                    if bank == 4:
                        pe.wait_ge(vaug_done, 4)
                    for t in range(TT):
                        m = pe.transpose(ps[0:last - first, bank, t * P:(t + 1) * P], mx[:, t, first:last], ident[:])
                    m.then_inc(turned, 1)

            def pv(b, par, s):
                g, kt = s // TT, s % TT
                pe.wait_ge(exp_done, 32 * b + 2 * s + 2)
                if kt == 0:
                    if g >= 2:
                        pe.wait_ge(y_evac, NG * b + g - 1)
                    elif later(b, 0, 1):
                        pe.wait_ge(x1_gated, b)
                for q in range(G):
                    m = pe.matmul(ps[32 * q:32 * q + 32, 4 + g % 2, :], vaug[par][:, kt, G * g + q, :], prob[:, s % 2, q, :],
                                  start=kt == 0, stop=kt == TT - 1, skip_group_check=True)
                m.then_inc(pv_done, 1)

            def transposed_scores(b, par, s, p):
                g, kt = s // TT, s % TT
                for q in (2 * p, 2 * p + 1):
                    m = pe.matmul(ps[:, q, :], kst[par][0:KROWS, G * g + q, kt * P:(kt + 1) * P],
                                  qst[par][0:KROWS, G * g + q, :], start=True, stop=True)
                m.then_inc(st_done, 1)

            def first_transposed(b, par):
                if later(b, 0, 1):
                    pe.wait_ge(m_loaded, 32 * (b + 1))
                else:
                    pe.wait_ge(half_loaded, 32)
                pe.wait_ge(part_l, 4 * (b + 2) if runs(b, 1) else 4 * NB)
                if later(b, 0, 2):
                    pe.wait_ge(o_gated, b - 1)
                for p in range(2):
                    transposed_scores(b, par, 0, p)

            def step(i, par):
                has_b, has_c, has_a, has_mlp = runs(i, 1), runs(i, 0), runs(i, 2), runs(i, -1)
                others = (lambda n: 0) if early(i) else (lambda n: n)
                if has_c:
                    if not later(i, 0, 1):
                        pe.wait_ge(const_set, 7)
                        first_transposed(i, par)
                    pe.wait_ge(vaug_done, 2 * (i + 2) if has_b else 2 * NB)
                    for s in range(STEPS):
                        old, new = c_blocks(i, s)

                        def between(first, last):
                            scores(i - 1, 1 - par, min(last, old) - first)
                            scores(i, par, min(last, old + new) - max(first, old))

                        if s == STEPS // 2 and not later(i, 0, 1):
                            pe.wait_ge(m_loaded, 32)
                        for p in range(2):
                            if s:
                                pe.wait_ge(exp_done, 32 * i + 2 * s - 1 + p)
                                transposed_scores(i, par, s, p)
                            if later(i, 0, 1):
                                between(p, p + 1)
                            elif p == 1:
                                between(0, 2)
                        if s:
                            pv(i, par, s - 1)
                        between(2, old + new)
                        if s == OLD_TURN and not later(i, 0, 1):
                            turn_maxima(i - 1, NH // 2, NH)
                    pe.wait_ge(exp_done, 32 * (i + 1))
                if has_a:
                    if later(i, 2, 1) and not has_c:
                        pe.wait_ge(rest_done, 4 * (i + 2))
                    transposes(0, i + 2, 2)
                if has_c:
                    pv(i, par, STEPS - 1)
                scores(i, par, others(TURN_BLOCKS[0]))
                if has_mlp and not final(i - 1):
                    transposes(1, i - 1, 0)
                scores(i, par, others(TURN_BLOCKS[1]))
                if has_a:
                    b = i + 2
                    if not later(i, 2, 1):
                        pe.wait_ge(w_split, 2)
                        pe.wait_ge(prep_dve, 7)
                    for w in range(2):
                        for m in range(2):
                            if w == 0 and has_c:
                                pe.wait_ge(y_evac, NG * (i + 1) + m - 1)
                            for k in range(KC):
                                if w == 0 and m == 0:
                                    pe.wait_ge(zh_done[0], 2 * b + k + 1)
                                for n in range(2):
                                    pe.matmul(ps[:, QK_BANKS[2 * w + m], :], wqkvo[n][:, w, k, m * P:(m + 1) * P], zh[0][:, k, :],
                                              start=k == 0 and n == 0, stop=False)
                        pe.wait_ge(zl_done[0], b + 1)
                        for m in range(2):
                            for k in range(KC):
                                last = pe.matmul(ps[:, QK_BANKS[2 * w + m], :], wqkvo[0][:, w, k, m * P:(m + 1) * P], zl[0][:, k, :],
                                                 start=False, stop=k == KC - 1)
                            last.then_inc(qk_done, 1)
                            scores(i, par, others(QK_BLOCKS[2 * w + m]))
                    for t in range(TT):
                        if t % 2 == 0:
                            pe.wait_ge(rest_done, 4 * b + t // 2 + 1)
                        for k in range(KC):
                            f = slice(t * P, (t + 1) * P)
                            m = three(ps[:, 4 + t // 2, (t % 2) * H:(t % 2 + 1) * H], zh[0][:, k, f], zl[0][:, k, f],
                                      wqkvo[0][:, 2, k, :], wqkvo[1][:, 2, k, :], k == 0 and t % 2 == 0)
                        if t % 2:
                            m.then_inc(v_done, 1)
                        scores(i, par, others(V_BLOCKS[t]))
                else:
                    scores(i, par, others(sum(QK_BLOCKS + V_BLOCKS)))

                def wo_products(bank):
                    pe.wait_ge(yh_done, i + 1)
                    for t in range(TT):
                        f = slice(t * P, (t + 1) * P)
                        for k in range(KC):
                            for n in range(2):
                                pe.matmul(ps[:, bank + t // 2, (t % 2) * H:(t % 2 + 1) * H], yh[:, k, f], wqkvo[n][:, 3, k, :],
                                          start=k == 0 and n == 0 and t % 2 == 0, stop=False, skip_group_check=True)
                    if not final(i):
                        first_transposed(i + 1, 1 - par)
                    pe.wait_ge(yl_done, i + 1)
                    for t in range(TT):
                        f = slice(t * P, (t + 1) * P)
                        for k in range(KC):
                            m = pe.matmul(ps[:, bank + t // 2, (t % 2) * H:(t % 2 + 1) * H], yl[:, k, f], wqkvo[0][:, 3, k, :],
                                          start=False, stop=k == KC - 1, skip_group_check=True)
                        if t % 2:
                            m.then_inc(wo_done, 1)

                if has_mlp:
                    b = i - 1

                    def up(j):
                        if j >= 2:
                            pe.wait_ge(gelu_done, JT * b + j - 1)
                        else:
                            if j == 0:
                                pe.wait_ge(zh_done[1], 2 * i)
                            if final(b):
                                pe.wait_ge(gelu_done, JT * b)
                            elif has_a:
                                pe.wait_ge(vaug_done, 2 * (i + 3) + j - 1)
                            else:
                                pe.wait_ge(y_evac, NG * (i + 1) + j - 1)
                        f = slice(j * P, (j + 1) * P)
                        for k in range(KC):
                            for n in range(2):
                                pe.matmul(ps[:, 4 + j % 2, :], w1[n][:, k, f], zh_of(1, b)[:, k, :], start=k == 0 and n == 0, stop=False)
                        if j == 0:
                            pe.wait_ge(zl_done[1], i)
                        for k in range(KC):
                            m = pe.matmul(ps[:, 4 + j % 2, :], w1[0][:, k, f], zl_of(1, b)[:, k, :], start=False, stop=k == KC - 1)
                        m.then_inc(w1_done, 1)

                    def down(j):
                        pe.wait_ge(hl_done, JT * b + j + 1)
                        if j == 0:
                            pe.wait_ge(rest_done, 4 * (i + 3) if has_a else 4 * NB)
                            if final(b):
                                pe.wait_ge(o_gated, b)
                        for t in range(TT):
                            f = slice(t * P, (t + 1) * P)
                            m = three(ps[:, t, 0:H], hh[:, j % HR, f], hl[:, j % HR, f], w2[0][:, j, :], w2[1][:, j, :],
                                      j == 0, j == JT - 1)
                        m.then_inc(w2_done, 1)

                    for j in range(3):
                        up(j)
                        scores(i, par, UP_BLOCKS[j])
                    for j in range(JT):
                        down(j)
                        scores(i, par, DOWN_BLOCKS[j])
                        if j == 5:
                            turn_maxima(i)
                        if j + 3 < JT:
                            up(j + 3)
                        if final(i) and j == WO_AT:
                            wo_products(6)
                        if final(i) and j == TURN_AT:
                            pe.wait_ge(x1_gated, NB)
                            transposes(1, i, 6)
                elif early(i):
                    scores(i, par, HALF + 2, (6, 7, 0, 1))
                    turn_maxima(i, 0, NH // 2, half_turned, 4)
                    scores(i, par, EXTRA - 2)
                else:
                    scores(i, par, tail_blocks(i))
                    turn_maxima(i)
                if has_c and not final(i):
                    if has_mlp:
                        pe.wait_ge(gelu_done, JT * i)
                    elif has_a:
                        pe.wait_ge(vaug_done, 2 * (i + 3))
                    wo_products(4)

            schedule(step, pe)

        @block.vector
        def _(dve):
            dve.wait_ge(prep_act, 1)
            e = z[0][:, 0, 0:KC * NB]
            dve.tensor_scalar(e, e, 1.0, None, ALU.add).then_inc(prep_dve, 1)
            dve.wait_ge(prep_dve, 1)
            dve.reciprocal(z[0][:, 0, 64:64 + KC * NB], e).then_inc(prep_dve, 1)
            dve.wait_ge(prep_dve, 2)
            dve.tensor_tensor(z[0][:, 1, 0:KC * NB], ps[:, 0, 0:KC * NB], z[0][:, 0, 64:64 + KC * NB], ALU.mult).then_inc(prep_dve, 1)

            def statistics(n, b, src, t):
                if t == 0:
                    if later(b, 0, 1):
                        dve.wait_ge(xn_done[n], b)
                    if n == 1:
                        dve.wait_ge(x1_done, b + 1)
                    else:
                        dve.wait_ge(xa_loaded, 16 * (b + 1))
                m = dve.bn_stats(stats[n][:, t, :], src[:, t, :])
                if t == TT - 1:
                    m.then_inc(stat_done[n], 1)

            def variance(n, b):
                dve.wait_ge(stat_done[n], 3 * b + 1)
                dve.memset(vare[n][:], EPS)
                for t in range(TT):
                    m = dve.bn_aggr(mv[n][:, t, :], stats[n][:, t, :])
                m.then_inc(stat_done[n], 1)
                dve.wait_ge(stat_done[n], 3 * b + 2)
                dve.tensor_tensor(vare[n][:], mv[n][:, :, 1], vare[n][:], ALU.add).then_inc(stat_done[n], 1)

            def normalise(n, b, src, t):
                if t == 0:
                    dve.wait_ge(rstd_done[n], b + 1)
                    if n == 1 and later(b, 0, 1) and not final(b):
                        dve.wait_ge(out_written, 16 * b)
                    dve.wait_ge(stat_done[n], 3 * b + 3)
                m = dve.tensor_scalar(xn_of(n, b)[:, t, :], src[:, t, :], mv[n][:, t, 0:1], rstd[n][:, t:t + 1],
                                      ALU.subtract, ALU.mult)
                if t == TT - 1:
                    m.then_inc(xn_done[n], 1)

            def norm_piece(n, b, src, k):
                if k < TT:
                    statistics(n, b, src, k)
                elif k == TT:
                    variance(n, b)
                elif k > TT:
                    normalise(n, b, src, k - TT - 1)

            for t in range(TT):
                statistics(0, 0, xa, t)
            variance(0, 0)
            dve.wait_ge(prep_pe, 2)
            dve.wait_ge(bc_loaded, 16)
            c6 = stage[0:NB, 1, 256:256 + 6 * H]
            dve.tensor_tensor(c6, ps[0:NB, 1:4, :].rearrange("p n f -> p (n f)"), c6, ALU.add).then_inc(prep_dve, 1)
            for t in range(TT):
                normalise(0, 0, xa, t)
            dve.wait_ge(prep_pe, 3)
            dve.tensor_copy(mod[:].rearrange("p n b -> p (n b)"), ps[:, 4, 0:12 * NB]).then_inc(prep_dve, 1)
            dve.wait_ge(prep_dve, 5)
            for n in (SC1, SC2):
                m = dve.tensor_scalar(mod[:, 2 * n:2 * n + 2, :], mod[:, 2 * n:2 * n + 2, :], 1.0, None, ALU.add)
            m.then_inc(prep_dve, 1)
            dve.wait_ge(wqkvo_loaded, 64)
            dve.tensor_copy(wqkvo[0][:].rearrange("p n c f -> p (n c f)"), stage[:, 0, :]).then_inc(w_split, 1)
            dve.wait_ge(w_split, 1)
            dve.tensor_tensor(wqkvo[1][:].rearrange("p n c f -> p (n c f)"), stage[:, 0, :],
                              wqkvo[0][:].rearrange("p n c f -> p (n c f)").bitcast(F32), ALU.subtract).then_inc(w_split, 1)
            dve.wait_ge(prep_pe, 4)
            dve.tensor_copy(bias_t[:], ps[:, 5, 0:3 * KC + JT]).then_inc(prep_dve, 1)
            dve.wait_ge(prep_dve, 7)

            block_at = [0]

            def row_max(i, blocks, banks=(6, 7)):
                if not runs(i, 1):
                    return
                for _ in range(blocks):
                    n = block_at[0]
                    block_at[0] = (n + 1) % (NH * TT)
                    if n == 0 and later(i, 1, 1):
                        dve.wait_ge(mt_done, i + 1)
                    dve.wait_ge(s_done, 64 * (i + 1) + n + 1)
                    h, t = n // TT, n % TT
                    dve.tensor_reduce(mx[:, t, h:h + 1], ps[:, banks[n % len(banks)], :], AXX, ALU.max).then_inc(max_done, 1)

            def z_hi(n, b):
                for k in range(KC):
                    dve.wait_ge(z_done[n], 2 * b + k + 1)
                    dve.tensor_copy(zh_of(n, b)[:, k, :], z_of(n, b)[:, k, :]).then_inc(zh_done[n], 1)

            def z_lo(n, b):
                dve.wait_ge(zh_done[n], 2 * (b + 1))
                dve.tensor_tensor(zl_of(n, b)[:], z_of(n, b)[:], zh_of(n, b)[:].bitcast(F32), ALU.subtract).then_inc(zl_done[n], 1)

            def maxima_rows(i, heads=NH, turned=mt_done, done=mrow_done, bank=6):
                if not runs(i, 1):
                    return
                if turned is mt_done:
                    dve.wait_ge(mt_done, i + 2)
                    if later(i, 1, 1):
                        dve.wait_ge(m_loaded, 32 * (i + 1))
                    else:
                        dve.wait_ge(half_loaded, 32)
                else:
                    dve.wait_ge(turned, 1)
                dve.tensor_copy(mrow[0:heads, 0, :], ps[0:heads, bank, :]).then_inc(done, 1)
                dve.wait_ge(done, 2 * (i + 1) + 1)
                dve.tensor_tensor(mrow[0:heads, 1, :], ps[0:heads, bank, :], mrow[0:heads, 0, :], ALU.subtract).then_inc(done, 1)

            def step(i, par):
                has_b, has_c, has_a, has_mlp = runs(i, 1), runs(i, 0), runs(i, 2), runs(i, -1)
                others = (lambda n: 0) if early(i) else (lambda n: n)
                ln2 = {2: (0, 1), 3: (2, 3), 4: (4,), 7: (5, 6), 8: (7, 8)}
                ln1 = {5: (0, 1), 6: (2, 3), 9: (4,), 12: (5, 6), 13: (7, 8)}
                for s in range(STEPS):
                    old, new = c_blocks(i, s)
                    for n in range(max(4, old)):
                        if has_c and n < old:
                            row_max(i - 1, 1)
                        elif has_c and n < old + new:
                            row_max(i, 1)
                        if n < 2:
                            if has_mlp and not final(i - 1):
                                for k in ln2.get(s, ())[n:n + 1]:
                                    norm_piece(1, i - 1, x1, k)
                            if has_a and later(i, 2, 2):
                                for k in ln1.get(s, ())[n:n + 1]:
                                    norm_piece(0, i + 2, xa, k)
                    if s == OLD_TURN and has_c and not later(i, 0, 1):
                        maxima_rows(i - 1, NH // 2)
                row_max(i, others(TURN_BLOCKS[0]))
                if has_a:
                    z_hi(0, i + 2)
                    z_lo(0, i + 2)
                if has_a and not later(i, 2, 1):
                    for t in range(TT):
                        statistics(0, 1, xa, t)
                    variance(0, 1)
                row_max(i, others(TURN_BLOCKS[1]))
                if has_mlp and not final(i - 1):
                    z_hi(1, i - 1)
                    if not has_a:
                        z_lo(1, i - 1)

                def rest_of(b, j):
                    dve.wait_ge(part_h, 4 * b + j + 1)
                    if j >= 2:
                        dve.wait_ge(part_l, 4 * b + j - 1)
                    elif early(i) and later(i, 2, 1):
                        dve.wait_ge(part_l, 4 * b + j - 1)
                    dve.scalar_tensor_tensor(out=rest[:, j % 2, :], in0=ps[:, QK_BANKS[j], :], scalar=bqk[:, j // 2, j % 2:j % 2 + 1],
                                             in1=parts[:, j, 0, :], op0=ALU.add, op1=ALU.subtract).then_inc(rest_done, 1)
                    dve.wait_ge(rest_done, 4 * b + j + 1)
                    dve.tensor_copy(parts[:, j, 1, :], rest[:, j % 2, :]).then_inc(part_m, 1)

                for j in range(4):
                    if j == 3:
                        row_max(i, others(QK_BLOCKS[3] + sum(V_BLOCKS[0:2])))
                    if has_a:
                        rest_of(i + 2, j)
                    if j == 3 and has_c:
                        dve.wait_ge(den_loaded, 16 * (i + 1))
                        dve.reciprocal(rec, den).then_inc(rec_done, 1)
                    if j < 3:
                        row_max(i, others(QK_BLOCKS[j]))
                row_max(i, others(sum(V_BLOCKS[2:4])))
                if has_a and not later(i, 2, 1):
                    for t in range(TT):
                        normalise(0, 1, xa, t)

                def y_norm(part):
                    if part == 0:
                        dve.wait_ge(yc_loaded, 32 * (i + 1))
                        dve.wait_ge(rb_loaded, 32 * (i + 1))
                        dve.tensor_tensor(yc[:], yc[:], rb[:], ALU.mult).then_inc(yn_done, 1)
                    if part == 1:
                        dve.wait_ge(v_done, 2 * (i + 3) if has_a else 2 * NB)
                        dve.wait_ge(yn_done, i + 1)
                        for k in range(KC):
                            m = dve.tensor_scalar(yh[:, k, :], yc[:, k, :], bv_t[:, k:k + 1], None, ALU.add)
                        m.then_inc(yh_done, 1)
                    if part == 2:
                        dve.wait_ge(yh_done, i + 1)
                        for k in range(KC):
                            m = dve.scalar_tensor_tensor(out=yl[:, k, :], in0=yc[:, k, :], scalar=bv_t[:, k:k + 1],
                                                         in1=yh[:, k, :].bitcast(F32), op0=ALU.add, op1=ALU.subtract)
                        m.then_inc(yl_done, 1)

                def residual(wo_out):
                    dve.wait_ge(wo_done, 2 * (i + 1))
                    dve.wait_ge(xg_done, i + 1)
                    if later(i, 0, 1) and not final(i):
                        dve.wait_ge(o_done, i)
                    dve.tensor_tensor(x1_of(i)[:], wo_out.rearrange("p n (t f) -> p (n t) f", t=2),
                                      ga[:].unsqueeze(1).broadcast_to([P, TT, H]), ALU.mult).then_inc(x1_gated, 1)
                    dve.wait_ge(x1_gated, i + 1)
                    dve.tensor_tensor(x1_of(i)[:], x1_of(i)[:], xd[:], ALU.add).then_inc(x1_done, 1)

                if has_mlp:
                    b = i - 1
                    row_max(i, UP_BLOCKS[0])
                    for j in range(JT):
                        dve.wait_ge(gelu_done, JT * b + j + 1)
                        if j >= HR:
                            dve.wait_ge(w2_done, JT * b + j - HR + 1)
                        elif later(i, -1, 1):
                            dve.wait_ge(w2_done, JT * b)
                        dve.tensor_copy(hh[:, j % HR, :], hb[:, j % HB, :]).then_inc(hh_done, 1)
                        if j + 1 < len(UP_BLOCKS):
                            row_max(i, UP_BLOCKS[j + 1])
                        elif j >= 2:
                            row_max(i, DOWN_BLOCKS[j - 2])
                        if j == JT - 1:
                            maxima_rows(i)
                        if j >= 5 and has_c and not final(i):
                            y_norm(j - 5)
                        if final(i) and j == WO_AT:
                            for part in range(3):
                                y_norm(part)
                        if final(i) and j == LN2_AT:
                            residual(ps[:, 6:8, :])
                            for t in range(TT):
                                statistics(1, i, xa, t)
                            variance(1, i)
                        if final(i) and j == LN2_AT + 1:
                            for t in range(TT):
                                normalise(1, i, xa, t)
                        if final(i) and j == JT - 1:
                            z_hi(1, i)
                            z_lo(1, i)
                    dve.wait_ge(w2_done, JT * i)
                    dve.tensor_tensor(osb[:], ps[:, 0:TT, 0:H], gm[:].unsqueeze(1).broadcast_to([P, TT, H]), ALU.mult).then_inc(o_gated, 1)
                    dve.wait_ge(o_gated, i)
                    dve.wait_ge(x1g_done, i)
                    dve.tensor_tensor(osb[:], osb[:], x1_of(b)[:], ALU.add).then_inc(o_done, 1)
                else:
                    if early(i):
                        row_max(i, HALF + 2, (6, 7, 0, 1))
                        maxima_rows(i, NH // 2, half_turned, half_rows, 4)
                        row_max(i, EXTRA - 2)
                    else:
                        row_max(i, tail_blocks(i))
                        maxima_rows(i)
                    if has_c:
                        for part in range(3):
                            y_norm(part)
                if has_c and not final(i):
                    residual(ps[:, 4:6, :])

            schedule(step, dve)


_INS = ["x", "cond_1024"] + ["L0_cond_" + n for n in ("Wc", "bc", "Wq", "bq", "Wk", "bk", "Wv", "bv", "Wo", "bo", "W1", "b1", "W2", "b2")]


def kernel(**inputs):
    import numpy as _np
    import concourse.bacc as _bacc
    from concourse import mybir as _mybir
    from concourse.bass_utils import run_bass_kernel_spmd as _run

    nc = _bacc.Bacc("TRN2", target_bir_lowering=False, num_devices=1)
    arrays, args = {}, []
    for name in _INS:
        a = _np.ascontiguousarray(inputs[name])
        arrays[f"in_{name}_dram"] = a
        args.append(nc.dram_tensor(f"in_{name}_dram", a.shape, _mybir.dt.from_np(a.dtype), kind="ExternalInput").ap())
    args.append(nc.dram_tensor("out_0_dram", (NB, S, H), _mybir.dt.float32, kind="ExternalOutput").ap())
    args.append(nc.dram_tensor("c6_scratch", (NB, 6 * H), _mybir.dt.float32).ap())
    args.append(nc.dram_tensor("parts_scratch", (2, 3, H, S), _mybir.dt.bfloat16).ap())
    args.append(nc.dram_tensor("y_scratch", (NH, 2 * DH, S), _mybir.dt.float32).ap())
    args.append(nc.dram_tensor("r_scratch", (NH, S), _mybir.dt.float32).ap())
    dit_block(nc, *args)
    r = _run(nc, [arrays], core_ids=[0])
    return r.results[0]["out_0_dram"]
```
